# Optimizing a Trainium2 kernel written in Bass

```python
import numpy as np
import jax
import jax.numpy as jnp

def _softmax(x, axis=-1):
    return jax.nn.softmax(x, axis=axis)
def _gelu(x):
    return jax.nn.gelu(x, approximate=True)
def _silu(x):
    return jax.nn.silu(x)
def _sigmoid(x):
    return jax.nn.sigmoid(x)
def _layernorm(x, axis=-1, eps=1e-5):
    m = jnp.mean(x, axis=axis, keepdims=True)
    v = jnp.var(x, axis=axis, keepdims=True)
    return (x - m) / jnp.sqrt(v + eps)
def _scatter_add(tgt, idx, src, axis=0):
    return tgt.at[idx].add(src)
def _segment_sum(src, seg, n):
    return jax.ops.segment_sum(src, seg, n)

kernel_name = 'mk_adj_preln_d4_adj_512_2d96b9'

def setup_inputs(seed: int = 0):
    np.random.seed(seed)
    _w = jnp.asarray
    def _rec_inputs():
        import jax
        import jax.numpy as jnp
        _gk = jax.random.key(seed)
        x = -0.0002928 + 1 * jax.random.normal(jax.random.fold_in(_gk, 1), (3327, 512), jnp.float32)
        _a = jax.random.bernoulli(jax.random.fold_in(_gk, 2), 0.00120228, (3327, 3327))
        adj = _a.astype(jnp.int32)
        return x, adj
    x, adj = _rec_inputs()
    def _L0_gnn_setup():
        import jax, jax.numpy as jnp
        import numpy as np
        N, D_IN, D_OUT = (8192, 512, 512)
        key = jax.random.key(seed)
        ks = jax.random.split(key, 8)
        scale_in = 1.0 / np.sqrt(D_IN)
        scale_cat = 1.0 / np.sqrt(2 * D_OUT)
        return {'x': jax.random.normal(ks[0], (N, D_IN), dtype=jnp.float32), 'adj': jax.random.randint(ks[1], (N, N), 0, 2, dtype=jnp.int32), 'W_self': jax.random.uniform(ks[2], (D_IN, D_OUT), jnp.float32, -scale_in, scale_in), 'b_self': jax.random.uniform(ks[3], (D_OUT,), jnp.float32, -scale_in, scale_in), 'W_nb': jax.random.uniform(ks[4], (D_IN, D_OUT), jnp.float32, -scale_in, scale_in), 'b_nb': jax.random.uniform(ks[5], (D_OUT,), jnp.float32, -scale_in, scale_in), 'W_comb': jax.random.uniform(ks[6], (2 * D_OUT, D_OUT), jnp.float32, -scale_cat, scale_cat), 'b_comb': jax.random.uniform(ks[7], (D_OUT,), jnp.float32, -scale_cat, scale_cat)}
    _L0_gnn_all = _L0_gnn_setup()
    _L0_gnn_in = {k: v for k, v in _L0_gnn_all.items() if k in ('W_self', 'b_self', 'W_nb', 'b_nb', 'W_comb', 'b_comb', )}
    del _L0_gnn_all

    def _L1_gnn_setup():
        import jax, jax.numpy as jnp
        import numpy as np
        NEG_INF = -9000000000000000.0
        key = jax.random.key(seed)
        k1, k2, k3, k4 = jax.random.split(key, 4)
        N, F_in, H, F_out = (4096, 512, 8, 64)
        node_features = jax.random.normal(k1, (N, F_in), dtype=jnp.float32)
        adj_matrix = jax.random.randint(k2, (N, N), 0, 2, dtype=jnp.int32)
        adj_matrix = jnp.maximum(adj_matrix, jnp.eye(N, dtype=jnp.int32))
        W = jax.random.normal(k3, (H, F_in, F_out), dtype=jnp.float32) * 0.05
        a = jax.random.normal(k4, (H, 2 * F_out), dtype=jnp.float32) * 0.05
        return {'node_features': node_features, 'adj_matrix': adj_matrix, 'W': W, 'a': a}
    _L1_gnn_all = _L1_gnn_setup()
    _L1_gnn_in = {k: v for k, v in _L1_gnn_all.items() if k in ('W', 'a', )}
    del _L1_gnn_all

    def _L2_gnn_setup():
        import jax, jax.numpy as jnp
        import numpy as np
        ALPHA = 0.2
        NEG_INF = -9000000000000000.0

        def make_quaternion_mul(kernel):
            r, i, j, k = jnp.split(kernel, 4, axis=1)
            r2 = jnp.concatenate([r, -i, -j, -k], axis=0)
            i2 = jnp.concatenate([i, r, -k, j], axis=0)
            j2 = jnp.concatenate([j, k, r, -i], axis=0)
            k2 = jnp.concatenate([k, -j, i, r], axis=0)
            return jnp.concatenate([r2, i2, j2, k2], axis=1)
        key = jax.random.key(seed)
        k1, k2, k3, k4 = jax.random.split(key, 4)
        N, IN, OUT, H = (4096, 512, 128, 4)
        x = jax.random.normal(k1, (N, IN), dtype=jnp.float32)
        adj = jax.random.randint(k2, (N, N), 0, 2, dtype=jnp.int32)
        stdv = float(np.sqrt(6.0 / (IN // 4 + OUT)))
        W = jax.random.uniform(k3, (H, IN // 4, OUT), dtype=jnp.float32, minval=-stdv, maxval=stdv)
        a_std = float(np.sqrt(2.0 / (2 * OUT + 1))) * 1.414
        a = jax.random.normal(k4, (H, 2 * OUT), dtype=jnp.float32) * a_std
        return {'x': x, 'adj': adj, 'W': W, 'a': a}
    _L2_gnn_all = _L2_gnn_setup()
    _L2_gnn_in = {k: v for k, v in _L2_gnn_all.items() if k in ('W', 'a', )}
    del _L2_gnn_all

    def _L3_gnn_setup():
        import jax, jax.numpy as jnp
        import numpy as np
        N = 8192
        IN_F = 512
        OUT_F = 512
        ALPHA = 0.2
        NEG_INF = -9000000000000000.0
        key = jax.random.key(seed)
        k1, k2, k3, k4, k5 = jax.random.split(key, 5)
        x = jax.random.normal(k1, (N, IN_F), dtype=jnp.float32)
        adj = jax.random.randint(k2, (N, N), 0, 2, dtype=jnp.int32)
        W = jax.random.normal(k3, (OUT_F, IN_F), dtype=jnp.float32) / np.sqrt(IN_F)
        a1 = jax.random.normal(k4, (OUT_F,), dtype=jnp.float32) / np.sqrt(2 * OUT_F)
        a2 = jax.random.normal(k5, (OUT_F,), dtype=jnp.float32) / np.sqrt(2 * OUT_F)
        return {'x': x, 'adj': adj, 'W': W, 'a1': a1, 'a2': a2}
    _L3_gnn_all = _L3_gnn_setup()
    _L3_gnn_in = {k: v for k, v in _L3_gnn_all.items() if k in ('W', 'a1', 'a2', )}
    del _L3_gnn_all

    return {
        "x": x,
        "adj": adj,
        "L0_gnn_W_self": _L0_gnn_in["W_self"],
        "L0_gnn_b_self": _L0_gnn_in["b_self"],
        "L0_gnn_W_nb": _L0_gnn_in["W_nb"],
        "L0_gnn_b_nb": _L0_gnn_in["b_nb"],
        "L0_gnn_W_comb": _L0_gnn_in["W_comb"],
        "L0_gnn_b_comb": _L0_gnn_in["b_comb"],
        "L1_gnn_W": _L1_gnn_in["W"],
        "L1_gnn_a": _L1_gnn_in["a"],
        "L2_gnn_W": _L2_gnn_in["W"],
        "L2_gnn_a": _L2_gnn_in["a"],
        "L3_gnn_W": _L3_gnn_in["W"],
        "L3_gnn_a1": _L3_gnn_in["a1"],
        "L3_gnn_a2": _L3_gnn_in["a2"],
    }

def reference(x, adj, L0_gnn_W_self, L0_gnn_b_self, L0_gnn_W_nb, L0_gnn_b_nb, L0_gnn_W_comb, L0_gnn_b_comb, L1_gnn_W, L1_gnn_a, L2_gnn_W, L2_gnn_a, L3_gnn_W, L3_gnn_a1, L3_gnn_a2):
    import jax
    import jax.numpy as jnp
    def _L0_gnn_ref(x, adj, W_self, b_self, W_nb, b_nb, W_comb, b_comb):
        import jax, jax.numpy as jnp
        import numpy as np
        N, D_IN, D_OUT = (8192, 512, 512)
        mask = (adj > 0).astype(x.dtype)
        deg = jnp.sum(mask, axis=1, keepdims=True)
        agg = mask @ x / jnp.maximum(deg, 1.0)
        self_f = x @ W_self + b_self
        nb_f = agg @ W_nb + b_nb
        combined = jnp.concatenate([self_f, nb_f], axis=-1)
        out = combined @ W_comb + b_comb
        return jax.nn.relu(out)

    def _L1_gnn_ref(node_features, adj_matrix, W, a):
        import jax, jax.numpy as jnp
        import numpy as np
        NEG_INF = -9000000000000000.0
        alpha = 0.2
        H, F_in, F_out = W.shape
        Wh = jnp.einsum('nf,hfo->hno', node_features, W)
        f_src = jnp.einsum('hno,ho->hn', Wh, a[:, :F_out])
        f_dst = jnp.einsum('hno,ho->hn', Wh, a[:, F_out:])
        e = jax.nn.leaky_relu(f_src[:, :, None] + f_dst[:, None, :], negative_slope=alpha)
        masked = jnp.where(adj_matrix[None, :, :] > 0, e, NEG_INF)
        attn = jax.nn.softmax(masked, axis=-1)
        h_prime = jnp.einsum('hnm,hmo->hno', attn, Wh)
        return jnp.transpose(h_prime, (1, 0, 2)).reshape(h_prime.shape[1], H * F_out)

    def _L2_gnn_ref(x, adj, W, a):
        import jax, jax.numpy as jnp
        import numpy as np
        ALPHA = 0.2
        NEG_INF = -9000000000000000.0

        def make_quaternion_mul(kernel):
            r, i, j, k = jnp.split(kernel, 4, axis=1)
            r2 = jnp.concatenate([r, -i, -j, -k], axis=0)
            i2 = jnp.concatenate([i, r, -k, j], axis=0)
            j2 = jnp.concatenate([j, k, r, -i], axis=0)
            k2 = jnp.concatenate([k, -j, i, r], axis=0)
            return jnp.concatenate([r2, i2, j2, k2], axis=1)
        N = x.shape[0]
        hamilton = jax.vmap(make_quaternion_mul)(W)
        h = jnp.einsum('nf,hfo->hno', x, hamilton)
        OUT = h.shape[-1]
        a_src, a_dst = (a[:, :OUT], a[:, OUT:])
        f_src = jnp.einsum('hno,ho->hn', h, a_src)
        f_dst = jnp.einsum('hno,ho->hn', h, a_dst)
        e = jax.nn.leaky_relu(f_src[:, :, None] + f_dst[:, None, :], ALPHA)
        e = jnp.where((adj > 0)[None, :, :], e, NEG_INF)
        attn = jax.nn.softmax(e, axis=-1)
        h_prime = jnp.einsum('hnm,hmo->hno', attn, h)
        out = jnp.transpose(h_prime, (1, 0, 2)).reshape(N, -1)
        return jax.nn.elu(out)

    def _L3_gnn_ref(x, adj, W, a1, a2):
        import jax, jax.numpy as jnp
        import numpy as np
        N = 8192
        IN_F = 512
        OUT_F = 512
        ALPHA = 0.2
        NEG_INF = -9000000000000000.0
        h = x @ W.T
        src = h @ a1
        dst = h @ a2
        e = jax.nn.leaky_relu(src[:, None] + dst[None, :], negative_slope=ALPHA)
        e = jnp.where(adj == 0, jnp.float32(NEG_INF), e)
        attention = jax.nn.softmax(e, axis=1)
        h_prime = attention @ h
        return h_prime

    h = jnp.maximum(_layernorm(x, axis=-1), 0.0)
    x = x + _L0_gnn_ref(h, adj, L0_gnn_W_self, L0_gnn_b_self, L0_gnn_W_nb, L0_gnn_b_nb, L0_gnn_W_comb, L0_gnn_b_comb)
    h = jnp.maximum(_layernorm(x, axis=-1), 0.0)
    x = x + _L1_gnn_ref(h, adj, L1_gnn_W, L1_gnn_a)
    h = jnp.maximum(_layernorm(x, axis=-1), 0.0)
    x = x + _L2_gnn_ref(h, adj, L2_gnn_W, L2_gnn_a)
    h = jnp.maximum(_layernorm(x, axis=-1), 0.0)
    x = x + _L3_gnn_ref(h, adj, L3_gnn_W, L3_gnn_a1, L3_gnn_a2)
    return x


_drawn_inputs = setup_inputs


def setup_inputs(seed=0):
    import zlib

    import numpy as np

    out = dict(_drawn_inputs(seed))
    spreads = {}
    factors = {'L0_gnn_b_self': 8.0,
     'L0_gnn_b_nb': 7.267,
     'L0_gnn_b_comb': 4.421,
     'L3_gnn_a1': 6.308,
     'L3_gnn_a2': 2.767}
    for name, (base, spread) in spreads.items():
        noise = np.random.default_rng([zlib.crc32(name.encode()), seed]).standard_normal(out[name].shape)
        drawn = base * np.exp(spread * noise) if base else spread * noise
        out[name] = jnp.asarray(drawn.astype(out[name].dtype))
    for name, factor in factors.items():
        out[name] = (out[name] * factor).astype(out[name].dtype)
    return out
```

```python
import concourse.bass as bass
from concourse import mybir
from contextlib import ExitStack

N, D, P = 3327, 512, 128
NT = 26
NEG = -9000000000000000.0
HEADS = [1, 8, 4, 1]
FP32 = mybir.dt.float32
I32 = mybir.dt.int32
ALU = mybir.AluOpType
ACT = mybir.ActivationFunctionType
AX = mybir.AxisListType


class Turns:

    def __init__(self, nc, ctx, name):
        self.sems = {(e, n): ctx.enter_context(nc.semaphore(f"{name}_{e}{n}")) for e in ENGINES for n in (1, 16)}
        self.items = []
        self.last = None

    def turn(self, engine, fn, amount=1):
        item = {"engine": engine, "fn": fn, "amount": amount, "wait": None, "to": None}
        if self.last is not None:
            n = self.last["amount"]
            self.last["to"] = item["wait"] = self.sems[engine, n]
        self.items.append(item)
        self.last = item

    def dma(self, fn):
        self.turn("sync", fn, 16)

    def loop(self, count, body):
        self.turn("sync", None)
        outer, self.items = self.items, []
        start = {"engine": "sync", "fn": None, "amount": 1, "wait": None, "to": None}
        self.items.append(start)
        self.last = start
        body()
        self.turn("sync", None)
        inner, self.items = self.items, outer
        self.items.append({"engine": "loop", "count": count, "items": inner})
        after = {"engine": "sync", "fn": None, "amount": 1, "wait": None, "to": None}
        self.items.append(after)
        self.last = after

    def emit(self, e, name, items=None, i=None):
        for item in self.items if items is None else items:
            if item["engine"] == "loop":
                if any(x["engine"] == name for x in item["items"]):
                    with e.Fori(0, item["count"]) as k:
                        self.emit(e, name, item["items"], k)
                continue
            if item["engine"] != name:
                continue
            if item["wait"] is not None:
                e.wait_ge(item["wait"], 16 if item["wait"] is self.sems[name, 16] else 1)
                e.sem_clear(item["wait"])
            last = item["fn"](e, i) if item["fn"] else None
            if item["to"] is not None:
                if last is None:
                    e.sem_inc(item["to"], 1)
                else:
                    last.then_inc(item["to"], item["amount"])


ENGINES = ["sync", "tensor", "vector", "scalar", "gpsimd"]


def rsqrt_steps(y, var, hv, t):
    guess = float(0x5F3759DF - (1 << 30) - (1 << 22))
    yield lambda e: e.tensor_scalar(hv, var, 1e-5, -0.5, ALU.add, ALU.mult)
    yield lambda e: e.tensor_scalar(y.bitcast(I32), hv.bitcast(I32), -0.5, guess, ALU.mult, ALU.add)
    for _ in range(3):
        yield lambda e: e.tensor_scalar(t, hv, y, y, ALU.mult, ALU.mult)
        yield lambda e: e.tensor_scalar(y, t, 1.5, y, ALU.add, ALU.mult)


def chain_prep(T, nc, g, dr):
    ident, A, B, C, ps = g["ident"], g["wa"], g["wb"], g["wc"], g["ps"]
    WE, row, pr = g["WE"], g["brow"], g["ps2"]

    def rows(x):
        return x.rearrange("(k p) o -> p k o", p=P)

    def transposed(dst, src):
        for k in range(4):
            def tr(e, i, k=k):
                for c in range(4):
                    last = e.transpose(ps[:, c * P:(c + 1) * P], src[:, c, k * P:(k + 1) * P], ident)
                return last
            T.turn("tensor", tr)
            T.turn("vector", lambda e, i, k=k: e.tensor_copy(dst[:, k, :], ps))

    for which, (w, b, half) in enumerate([("W_nb", "b_nb", 1), ("W_self", "b_self", 0)]):
        T.dma(lambda e, i, w=w: e.dma_start(A, rows(dr[w])))
        T.dma(lambda e, i, half=half: e.dma_start(B, rows(dr["W_comb"][half * D:(half + 1) * D, :])))
        T.dma(lambda e, i, b=b: e.dma_start(g["bcol"], dr[b].rearrange("(k p) -> p k", p=P), allow_slow_non_contiguous=True))
        transposed(C, A)
        for k in range(4):
            def mm(e, i, k=k):
                for c in range(4):
                    last = e.matmul(ps, C[:, c, k * P:(k + 1) * P], B[:, c, :], start=c == 0, stop=c == 3)
                return last
            T.turn("tensor", mm)
            T.turn("vector", lambda e, i, k=k: e.tensor_copy(A[:, k, :], ps))
        T.dma(lambda e, i, which=which: e.dma_start(dr["PW"][which], A.rearrange("p k o -> p (k o)")))

        def mb(e, i, which=which):
            for c in range(4):
                last = e.matmul(pr[0:1, :], g["bcol"][:, c:c + 1], B[:, c, :],
                                start=which == 0 and c == 0, stop=which == 1 and c == 3)
            return last
        T.turn("tensor", mb)
    T.dma(lambda e, i: e.dma_start(row[0:1, 1, :], dr["b_comb"].rearrange("(a n) -> a n", a=1)))
    T.turn("vector", lambda e, i: e.tensor_tensor(row[0:1, 0, :], pr[0:1, :], row[0:1, 1, :], ALU.add))
    T.dma(lambda e, i: e.dma_start(dr["PB"], row[0:1, 0, :]))

    def scores(l):
        F = D // HEADS[l]
        for s in range(2):
            if l < 3:
                src = dr[f"a{l}"][:, s * F:(s + 1) * F].rearrange("(q h) o -> q h o", q=1)
                dst = row[0:1, 0, :].rearrange("q (h o) -> q h o", o=F)
            else:
                src, dst = dr[f"a3{s}"].rearrange("(q o) -> q o", q=1), row[0:1, 0, :]
            T.dma(lambda e, i, src=src, dst=dst: e.dma_start(dst, src))
            T.turn("tensor", lambda e, i: e.matmul(ps, g["ones"][0:1, :], row[0:1, 0, :], start=True, stop=True))
            for k in range(4):
                T.turn("vector", lambda e, i, k=k: e.tensor_tensor(C[:, k, :], A[:, k, :], ps, ALU.mult))
            T.turn("vector", lambda e, i, s=s: e.tensor_reduce(
                WE[:, l - 1, :, s * 8:s * 8 + HEADS[l]],
                C.rearrange("p k (h o) -> p k h o", o=F), AX.X, ALU.add))
        T.dma(lambda e, i: e.dma_start(dr["PW"][l + 1], A.rearrange("p k o -> p (k o)")))

    for h in range(8):
        T.dma(lambda e, i, h=h: e.dma_start(A[:, :, h * 64:(h + 1) * 64],
                                            dr["W1"][h].rearrange("(k p) o -> p k o", p=P)))
    scores(1)
    T.dma(lambda e, i: e.dma_start(B[:, :, 0:P], dr["W2"].rearrange("h p o -> p h o")))
    parts = [[(0, 1), (1, -1), (2, -1), (3, -1)], [(1, 1), (0, 1), (3, -1), (2, 1)],
             [(2, 1), (3, 1), (0, 1), (1, -1)], [(3, 1), (2, -1), (1, 1), (0, 1)]]
    for q in range(4):
        for b in range(4):
            c, sign = parts[q][b]
            dst = A[:, b, :].rearrange("p (h q o) -> p h q o", h=4, q=4)[:, :, q, :]
            T.turn("vector", lambda e, i, dst=dst, c=c, sign=sign: e.tensor_scalar(
                dst, B[:, :, c * 32:(c + 1) * 32], float(sign), None, ALU.mult))
    scores(2)
    T.dma(lambda e, i: e.dma_start(B, rows(dr["W3"])))
    transposed(A, B)
    scores(3)


def chain_dense(T, nc, g, dr):
    f = g["f"]
    ident, ps, ps2, ps3 = g["ident"], g["ps"], g["ps2"], g["ps3"]
    WE = g["WE"]
    hT = f(0, 4 * N).rearrange("p (k n) -> p k n", n=N)
    WH = f(13312, 26 * D).rearrange("p (t o) -> p t o", o=D)
    base = 13312 * 2
    DB, U = f(base, N), f(base + 3328, N)
    ADJ = f(base + 6656, N).bitcast(I32)
    V = f(base + 9984, N)
    PT = f(base + 13312, NT * P).rearrange("p (t i) -> p t i", i=P)
    base += 13312 + NT * P
    assert base <= g["arena_words"], base
    x0 = base - NT * P
    b2 = 13312 * 2
    XT, YT, VT, H, HT, BI = (f(b2 + D * k, D) for k in range(6))
    W = f(b2 + 3328, 4 * D).rearrange("p (k o) -> p k o", k=4)
    W2 = f(b2 + 3328 + 4 * D, 4 * D).rearrange("p (k o) -> p k o", k=4)
    st = g["small"]
    WDB = f(x0, 4 * P).rearrange("p (k i) -> p k i", i=P)

    def at(e, i):
        return bass.ds(nc.s_assert_within(i * P - ((i + 7) >> 5), 0, N - P, skip_runtime_bounds_check_because="i < 26"), P)

    def add_layer(l, to):
        T.dma(lambda e, i: e.dma_start(XT, (dr["x"] if l <= 1 else dr["XS"][l - 2])[at(e, i), :]))
        if l == 0:
            return
        T.dma(lambda e, i: e.dma_start(YT, dr["Y"][at(e, i), :]))
        if l == 1:
            T.dma(lambda e, i: e.dma_start(VT, dr["V"][at(e, i), :]))
            T.turn("vector", lambda e, i: e.tensor_tensor(YT, YT, VT, ALU.add))
            T.turn("vector", lambda e, i: e.tensor_scalar(YT, YT, 0.0, None, ALU.max))
        if l == 3:
            T.turn("vector", lambda e, i: e.tensor_scalar(VT, YT, 0.0, None, ALU.min))
            T.turn("scalar", lambda e, i: e.activation(VT, VT, ACT.Exp))
            T.turn("vector", lambda e, i: e.tensor_scalar(YT, YT, 0.0, -1.0, ALU.max, ALU.add))
            T.turn("vector", lambda e, i: e.tensor_tensor(YT, YT, VT, ALU.add))
        T.turn("vector", lambda e, i: e.tensor_tensor(XT, XT, YT, ALU.add))
        T.dma(lambda e, i: e.dma_start(to[at(e, i), :], XT))

    for l in range(4):
        NH, F = HEADS[l], D // HEADS[l]
        T.dma(lambda e, i, l=l: e.dma_start(W.rearrange("p k o -> p (k o)"), dr["PW"][0 if l == 0 else l + 1]))
        if l == 0:
            T.dma(lambda e, i: e.dma_start(W2.rearrange("p k o -> p (k o)"), dr["PW"][1]))
            T.dma(lambda e, i: e.dma_start(g["brow"][0:1, 0, :], dr["PB"]))
            T.turn("tensor", lambda e, i: e.matmul(ps, g["ones"][0:1, :], g["brow"][0:1, 0, :], start=True, stop=True))
            T.turn("vector", lambda e, i: e.tensor_copy(BI, ps))

        def nodes(l=l, NH=NH):
            add_layer(l, dr["XS"][l - 1] if l else None)
            T.turn("vector", lambda e, i: e.bn_stats(st[:, 0:6], XT))
            T.turn("vector", lambda e, i: e.bn_aggr(st[:, 6:8], st[:, 0:6]))
            for fn in rsqrt_steps(st[:, 8:9], st[:, 7:8], st[:, 13:14], st[:, 14:15]):
                T.turn("vector", lambda e, i, fn=fn: fn(e))
            T.turn("vector", lambda e, i: e.scalar_tensor_tensor(st[:, 9:10], st[:, 6:7], -1.0, st[:, 8:9], ALU.mult, ALU.mult))
            T.turn("scalar", lambda e, i: e.activation(H, XT, ACT.Relu, bias=st[:, 9:10], scale=st[:, 8:9]))

            def tr(e, i):
                for k in range(4):
                    last = e.transpose(ps[:, k * P:(k + 1) * P], H[:, k * P:(k + 1) * P], ident)
                return last
            T.turn("tensor", tr)
            T.turn("vector", lambda e, i: e.tensor_copy(HT, ps))
            for k in range(4):
                T.dma(lambda e, i, k=k: e.dma_start(dr["HT"][k, :, at(e, i)], HT[:, k * P:(k + 1) * P]))

            def product(w, n, to):
                def mm(e, i):
                    for k in range(4):
                        last = e.matmul(ps[:, 0:n], HT[:, k * P:(k + 1) * P], w(k), start=k == 0, stop=k == 3)
                    return last
                T.turn("tensor", mm)
            product(lambda k: W[:, k, :], D, None)
            T.turn("vector", lambda e, i: e.tensor_copy(YT, ps))
            T.dma(lambda e, i: e.dma_start(dr["WH"][at(e, i), :], YT))
            if l == 0:
                product(lambda k: W2[:, k, :], D, None)
                T.turn("vector", lambda e, i: e.tensor_tensor(YT, ps, BI, ALU.add))
                T.dma(lambda e, i: e.dma_start(dr["V"][at(e, i), :], YT))
            else:
                product(lambda k: WE[:, l - 1, k, 0:NH], NH, None)
                T.turn("vector", lambda e, i: e.tensor_copy(st[:, 16:16 + NH], ps[:, 0:NH]))
                T.dma(lambda e, i: e.dma_start(dr["S"][at(e, i), 0:NH], st[:, 16:16 + NH], allow_slow_non_contiguous=True))

        T.loop(NT, nodes)
        for k in range(4):
            T.dma(lambda e, i, k=k: e.dma_start(hT[:, k, :], dr["HT"][k, :, 0:N]))
        T.dma(lambda e, i: e.dma_start(WH[:, 0:NT - 1, :], dr["WH"][0:(NT - 1) * P, :].rearrange("(t p) o -> p t o", p=P)))
        T.dma(lambda e, i: e.dma_start(WH[0:N - (NT - 1) * P, NT - 1, :], dr["WH"][(NT - 1) * P:N, :]))

        for h in range(NH):
            if l:
                T.turn("vector", lambda e, i, l=l, h=h: e.tensor_copy(
                    WDB, WE[:, l - 1, :, 8 + h:9 + h].broadcast_to([P, 4, P])))
                for j in range(0, N, D):
                    n = min(D, N - j)

                    def db(e, i, j=j, n=n):
                        for k in range(4):
                            last = e.matmul(ps[:, 0:n], WDB[:, k, :], hT[:, k, j:j + n], start=k == 0, stop=k == 3)
                        return last
                    T.turn("tensor", db)
                    T.turn("vector", lambda e, i, j=j, n=n: e.tensor_copy(DB[:, j:j + n], ps[:, 0:n]))

            def rows(l=l, h=h, F=F):
                T.dma(lambda e, i: e.dma_start(ADJ, dr["adj"][at(e, i), :]))
                if l == 0:
                    T.turn("vector", lambda e, i: e.tensor_scalar(U, ADJ, 0.0, None, ALU.is_gt))
                    T.turn("vector", lambda e, i: e.tensor_reduce(st[:, 10:11], U, AX.X, ALU.add))
                    T.turn("vector", lambda e, i: e.tensor_scalar(st[:, 10:11], st[:, 10:11], 1.0, None, ALU.max))
                else:
                    T.dma(lambda e, i: e.dma_start(st[:, 15:16], dr["S"][at(e, i), h:h + 1], allow_slow_non_contiguous=True))
                    T.turn("vector", lambda e, i: e.tensor_scalar(U, DB, st[:, 15:16], None, ALU.add))
                    T.turn("vector", lambda e, i: e.scalar_tensor_tensor(U, U, 0.2, U, ALU.mult, ALU.max))
                    if l < 3:
                        T.turn("vector", lambda e, i: e.scalar_tensor_tensor(U, ADJ, 0.0, U, ALU.is_gt, ALU.mult))
                        T.turn("vector", lambda e, i: e.tensor_scalar(V, ADJ, 0.0, NEG, ALU.is_le, ALU.mult))
                    else:
                        T.turn("vector", lambda e, i: e.scalar_tensor_tensor(U, ADJ, 0.0, U, ALU.not_equal, ALU.mult))
                        T.turn("vector", lambda e, i: e.tensor_scalar(V, ADJ, 0.0, NEG, ALU.is_equal, ALU.mult))
                    T.turn("vector", lambda e, i: e.tensor_tensor(U, U, V, ALU.add))
                    T.turn("vector", lambda e, i: e.tensor_reduce(st[:, 11:12], U, AX.X, ALU.max))
                    T.turn("vector", lambda e, i: e.tensor_scalar(st[:, 11:12], st[:, 11:12], -1.0, None, ALU.mult))
                    T.turn("scalar", lambda e, i: e.activation(U, U, ACT.Exp, bias=st[:, 11:12], accum_out=st[:, 10:11]))
                T.turn("vector", lambda e, i: e.reciprocal(st[:, 12:13], st[:, 10:11]))
                for c in range(0, NT, 4):
                    js = [(j, min(P, N - j * P)) for j in range(c, min(c + 4, NT))]

                    def tr(e, i, js=js, c=c):
                        for j, n in js:
                            last = e.transpose(ps[0:n, (j - c) * P:(j - c + 1) * P], U[:, j * P:j * P + n], ident)
                        return last
                    T.turn("tensor", tr)
                    full = [j for j, n in js if n == P]
                    T.turn("vector", lambda e, i, c=c, m=len(full): e.tensor_copy(
                        PT[:, c:c + m, :], ps[:, 0:m * P].rearrange("p (t i) -> p t i", i=P)))
                    for j, n in js[len(full):]:
                        T.turn("vector", lambda e, i, j=j, n=n, c=c: e.tensor_copy(
                            PT[0:n, j, :], ps[0:n, (j - c) * P:(j - c + 1) * P]))

                def mm(e, i):
                    for j in range(NT):
                        n = min(P, N - j * P)
                        last = e.matmul(ps2[:, 0:F], PT[0:n, j, :], WH[0:n, j, h * F:(h + 1) * F],
                                        start=j == 0, stop=j == NT - 1)
                    return last
                T.turn("tensor", mm)
                T.turn("vector", lambda e, i: e.tensor_scalar(V[:, 0:F], ps2[:, 0:F], st[:, 12:13], None, ALU.mult))
                T.dma(lambda e, i: e.dma_start(dr["Y"][at(e, i), h * F:(h + 1) * F], V[:, 0:F]))

            T.loop(NT, rows)
    T.loop(NT, lambda: add_layer(4, dr["out"]))


_W = {"W_self": "L0_gnn_W_self", "b_self": "L0_gnn_b_self", "W_nb": "L0_gnn_W_nb", "b_nb": "L0_gnn_b_nb",
      "W_comb": "L0_gnn_W_comb", "b_comb": "L0_gnn_b_comb", "W1": "L1_gnn_W", "a1": "L1_gnn_a",
      "W2": "L2_gnn_W", "a2": "L2_gnn_a", "W3": "L3_gnn_W", "a30": "L3_gnn_a1", "a31": "L3_gnn_a2"}


def program(nc, ins, out):
    dr = {k: ins[v] for k, v in _W.items()}
    dr.update(x=ins["x"], adj=ins["adj"], out=out)
    with ExitStack() as ctx:
        def scratch(name, shape):
            return nc.dram_tensor(name, shape, FP32, kind="Internal").ap()
        dr["PW"] = scratch("PW", [5, P, 4 * D])
        dr["PB"] = scratch("PB", [1, D])
        dr["XS"] = scratch("XS", [3, N, D])
        dr["Y"] = scratch("Y", [N, D])
        dr["V"] = scratch("V", [N, D])
        dr["WH"] = scratch("WH", [N, D])
        dr["HT"] = scratch("HT", [4, P, N])
        dr["S"] = scratch("S", [N, 8])
        words = 44000
        arena = ctx.enter_context(nc.sbuf_tensor("arena", [P, words], FP32))
        misc = ctx.enter_context(nc.sbuf_tensor("misc", [P, 1024 + 3 * 64 + 512], FP32))
        psum = ctx.enter_context(nc.psum_tensor("psum", [P, 8, D], FP32))

        def f(o, n):
            return arena[:, o:o + n]
        g = {"f": f, "arena_words": words, "ident": misc[:, 0:128], "ones": misc[:, 128:256],
             "WE": misc[:, 256:448].rearrange("p (l k h) -> p l k h", l=3, k=4),
             "bcol": misc[:, 448:452], "small": misc[:, 460:500],
             "brow": misc[:, 512:1536].rearrange("p (a n) -> p a n", a=2),
             "wa": f(0, 2048).rearrange("p (k o) -> p k o", k=4), "wb": f(2048, 2048).rearrange("p (k o) -> p k o", k=4),
             "wc": f(4096, 2048).rearrange("p (k o) -> p k o", k=4),
             "ps": psum[:, 0, :], "ps2": psum[:, 1, :], "ps3": psum[:, 2, :]}
        T = Turns(nc, ctx, "turn")
        T.turn("gpsimd", lambda e, i: e.memset(g["ident"], 0.0))
        T.turn("gpsimd", lambda e, i: e.memset(g["ones"], 1.0))
        T.turn("gpsimd", lambda e, i: e.affine_select(out=g["ident"], in_=g["ident"], compare_op=ALU.not_equal,
                                                      fill=1.0, base=0, pattern=[[-1, P]], channel_multiplier=1))
        chain_prep(T, nc, g, dr)
        chain_dense(T, nc, g, dr)
        block = ctx.enter_context(nc.Block())
        for name in ENGINES:
            {"sync": block.sync, "tensor": block.tensor, "vector": block.vector, "scalar": block.scalar, "gpsimd": block.gpsimd}[name](
                lambda e, name=name: T.emit(e, name))


_INS = ["x", "adj", *_W.values()]


def kernel(**inputs):
    import numpy as _np
    import concourse.bacc as _bacc
    from concourse import mybir as _mybir
    from concourse.bass_utils import run_bass_kernel_spmd as _run

    nc = _bacc.Bacc("TRN2", target_bir_lowering=False, num_devices=1)
    arrays, args = {}, {}
    for name in _INS:
        a = _np.ascontiguousarray(inputs[name])
        arrays[f"in_{name}"] = a
        args[name] = nc.dram_tensor(f"in_{name}", a.shape, _mybir.dt.from_np(a.dtype), kind="ExternalInput").ap()
    out = nc.dram_tensor("out_0", (N, D), _mybir.dt.float32, kind="ExternalOutput").ap()
    program(nc, args, out)
    r = _run(nc, [arrays], core_ids=[0])
    return r.results[0]["out_0"]
```

```python
import concourse.bass as bass
from concourse import mybir
from contextlib import ExitStack

N, D, P = 3327, 512, 128
NT = 26
NEG = -9000000000000000.0
HEADS = [1, 8, 4, 1]
FP32 = mybir.dt.float32
I32 = mybir.dt.int32
ALU = mybir.AluOpType
ACT = mybir.ActivationFunctionType
AX = mybir.AxisListType


class Turns:

    def __init__(self, nc, ctx, name):
        self.sems = {(e, n): ctx.enter_context(nc.semaphore(f"{name}_{e}{n}")) for e in ENGINES for n in (1, 16)}
        self.items = []
        self.last = None

    def turn(self, engine, fn, amount=1):
        item = {"engine": engine, "fn": fn, "amount": amount, "wait": None, "to": None}
        if self.last is not None:
            n = self.last["amount"]
            self.last["to"] = item["wait"] = self.sems[engine, n]
        self.items.append(item)
        self.last = item

    def dma(self, fn):
        self.turn("sync", fn, 16)

    def loop(self, count, body):
        self.turn("sync", None)
        outer, self.items = self.items, []
        start = {"engine": "sync", "fn": None, "amount": 1, "wait": None, "to": None}
        self.items.append(start)
        self.last = start
        body()
        self.turn("sync", None)
        inner, self.items = self.items, outer
        self.items.append({"engine": "loop", "count": count, "items": inner})
        after = {"engine": "sync", "fn": None, "amount": 1, "wait": None, "to": None}
        self.items.append(after)
        self.last = after

    def emit(self, e, name, items=None, i=None):
        for item in self.items if items is None else items:
            if item["engine"] == "loop":
                if any(x["engine"] == name for x in item["items"]):
                    with e.Fori(0, item["count"]) as k:
                        self.emit(e, name, item["items"], k)
                continue
            if item["engine"] != name:
                continue
            if item["wait"] is not None:
                e.wait_ge(item["wait"], 16 if item["wait"] is self.sems[name, 16] else 1)
                e.sem_clear(item["wait"])
            last = item["fn"](e, i) if item["fn"] else None
            if item["to"] is not None:
                if last is None:
                    e.sem_inc(item["to"], 1)
                else:
                    last.then_inc(item["to"], item["amount"])


ENGINES = ["sync", "tensor", "vector", "scalar", "gpsimd"]


def rsqrt_steps(y, var, hv, t):
    guess = float(0x5F3759DF - (1 << 30) - (1 << 22))
    yield lambda e: e.tensor_scalar(hv, var, 1e-5, -0.5, ALU.add, ALU.mult)
    yield lambda e: e.tensor_scalar(y.bitcast(I32), hv.bitcast(I32), -0.5, guess, ALU.mult, ALU.add)
    for _ in range(3):
        yield lambda e: e.tensor_scalar(t, hv, y, y, ALU.mult, ALU.mult)
        yield lambda e: e.tensor_scalar(y, t, 1.5, y, ALU.add, ALU.mult)


def chain_prep(T, nc, g, dr):
    ident, A, B, C, ps = g["ident"], g["wa"], g["wb"], g["wc"], g["ps"]
    WE, row, pr = g["WE"], g["brow"], g["ps2"]

    def rows(x):
        return x.rearrange("(k p) o -> p k o", p=P)

    def transposed(dst, src):
        for k in range(4):
            def tr(e, i, k=k):
                for c in range(4):
                    last = e.transpose(ps[:, c * P:(c + 1) * P], src[:, c, k * P:(k + 1) * P], ident)
                return last
            T.turn("tensor", tr)
            T.turn("vector", lambda e, i, k=k: e.tensor_copy(dst[:, k, :], ps))

    for which, (w, b, half) in enumerate([("W_nb", "b_nb", 1), ("W_self", "b_self", 0)]):
        T.dma(lambda e, i, w=w: e.dma_start(A, rows(dr[w])))
        T.dma(lambda e, i, half=half: e.dma_start(B, rows(dr["W_comb"][half * D:(half + 1) * D, :])))
        T.dma(lambda e, i, b=b: e.dma_start(g["bcol"], dr[b].rearrange("(k p) -> p k", p=P), allow_slow_non_contiguous=True))
        transposed(C, A)
        for k in range(4):
            def mm(e, i, k=k):
                for c in range(4):
                    last = e.matmul(ps, C[:, c, k * P:(k + 1) * P], B[:, c, :], start=c == 0, stop=c == 3)
                return last
            T.turn("tensor", mm)
            T.turn("vector", lambda e, i, k=k: e.tensor_copy(A[:, k, :], ps))
        T.dma(lambda e, i, which=which: e.dma_start(dr["PW"][which], A.rearrange("p k o -> p (k o)")))

        def mb(e, i, which=which):
            for c in range(4):
                last = e.matmul(pr[0:1, :], g["bcol"][:, c:c + 1], B[:, c, :],
                                start=which == 0 and c == 0, stop=which == 1 and c == 3)
            return last
        T.turn("tensor", mb)
    T.dma(lambda e, i: e.dma_start(row[0:1, 1, :], dr["b_comb"].rearrange("(a n) -> a n", a=1)))
    T.turn("vector", lambda e, i: e.tensor_tensor(row[0:1, 0, :], pr[0:1, :], row[0:1, 1, :], ALU.add))
    T.dma(lambda e, i: e.dma_start(dr["PB"], row[0:1, 0, :]))

    def scores(l):
        F = D // HEADS[l]
        for s in range(2):
            if l < 3:
                src = dr[f"a{l}"][:, s * F:(s + 1) * F].rearrange("(q h) o -> q h o", q=1)
                dst = row[0:1, 0, :].rearrange("q (h o) -> q h o", o=F)
            else:
                src, dst = dr[f"a3{s}"].rearrange("(q o) -> q o", q=1), row[0:1, 0, :]
            T.dma(lambda e, i, src=src, dst=dst: e.dma_start(dst, src))
            T.turn("tensor", lambda e, i: e.matmul(ps, g["ones"][0:1, :], row[0:1, 0, :], start=True, stop=True))
            for k in range(4):
                T.turn("vector", lambda e, i, k=k: e.tensor_tensor(C[:, k, :], A[:, k, :], ps, ALU.mult))
            T.turn("vector", lambda e, i, s=s: e.tensor_reduce(
                WE[:, l - 1, :, 8 - s * 8:8 - s * 8 + HEADS[l]],
                C.rearrange("p k (h o) -> p k h o", o=F), AX.X, ALU.add))
        T.dma(lambda e, i: e.dma_start(dr["PW"][l + 1], A.rearrange("p k o -> p (k o)")))

    for h in range(8):
        T.dma(lambda e, i, h=h: e.dma_start(A[:, :, h * 64:(h + 1) * 64],
                                            dr["W1"][h].rearrange("(k p) o -> p k o", p=P)))
    scores(1)
    T.dma(lambda e, i: e.dma_start(B[:, :, 0:P], dr["W2"].rearrange("h p o -> p h o")))
    parts = [[(0, 1), (1, -1), (2, -1), (3, -1)], [(1, 1), (0, 1), (3, -1), (2, 1)],
             [(2, 1), (3, 1), (0, 1), (1, -1)], [(3, 1), (2, -1), (1, 1), (0, 1)]]
    for q in range(4):
        for b in range(4):
            c, sign = parts[q][b]
            dst = A[:, b, :].rearrange("p (h q o) -> p h q o", h=4, q=4)[:, :, q, :]
            T.turn("vector", lambda e, i, dst=dst, c=c, sign=sign: e.tensor_scalar(
                dst, B[:, :, c * 32:(c + 1) * 32], float(sign), None, ALU.mult))
    scores(2)
    T.dma(lambda e, i: e.dma_start(B, rows(dr["W3"])))
    transposed(A, B)
    scores(3)


def chain_dense(T, nc, g, dr):
    f = g["f"]
    ident, ps, ps2, ps3 = g["ident"], g["ps"], g["ps2"], g["ps3"]
    WE = g["WE"]
    hT = f(0, 4 * N).rearrange("p (k n) -> p k n", n=N)
    WH = f(13312, 26 * D).rearrange("p (t o) -> p t o", o=D)
    base = 13312 * 2
    DB, U = f(base, N), f(base + 3328, N)
    ADJ = f(base + 6656, N).bitcast(I32)
    V = f(base + 9984, N)
    PT = f(base + 13312, NT * P).rearrange("p (t i) -> p t i", i=P)
    base += 13312 + NT * P
    assert base <= g["arena_words"], base
    x0 = base - NT * P
    b2 = 13312 * 2
    XT, YT, VT, H, HT, BI = (f(b2 + D * k, D) for k in range(6))
    W = f(b2 + 3328, 4 * D).rearrange("p (k o) -> p k o", k=4)
    W2 = f(b2 + 3328 + 4 * D, 4 * D).rearrange("p (k o) -> p k o", k=4)
    st = g["small"]
    WDB = f(x0, 4 * P).rearrange("p (k i) -> p k i", i=P)

    def at(e, i):
        return bass.ds(nc.s_assert_within(i * P - ((i + 7) >> 5), 0, N - P, skip_runtime_bounds_check_because="i < 26"), P)

    def add_layer(l, to):
        T.dma(lambda e, i: e.dma_start(XT, (dr["x"] if l <= 1 else dr["XS"][l - 2])[at(e, i), :]))
        if l == 0:
            return
        T.dma(lambda e, i: e.dma_start(YT, dr["Y"][at(e, i), :]))
        if l == 1:
            T.dma(lambda e, i: e.dma_start(VT, dr["V"][at(e, i), :]))
            T.turn("vector", lambda e, i: e.tensor_tensor(YT, YT, VT, ALU.add))
            T.turn("vector", lambda e, i: e.tensor_scalar(YT, YT, 0.0, None, ALU.max))
        if l == 3:
            T.turn("vector", lambda e, i: e.tensor_scalar(VT, YT, 0.0, None, ALU.min))
            T.turn("scalar", lambda e, i: e.activation(VT, VT, ACT.Exp))
            T.turn("vector", lambda e, i: e.tensor_scalar(YT, YT, 0.0, -1.0, ALU.max, ALU.add))
            T.turn("vector", lambda e, i: e.tensor_tensor(YT, YT, VT, ALU.add))
        T.turn("vector", lambda e, i: e.tensor_tensor(XT, XT, YT, ALU.add))
        T.dma(lambda e, i: e.dma_start(to[at(e, i), :], XT))

    for l in range(4):
        NH, F = HEADS[l], D // HEADS[l]
        T.dma(lambda e, i, l=l: e.dma_start(W.rearrange("p k o -> p (k o)"), dr["PW"][0 if l == 0 else l + 1]))
        if l == 0:
            T.dma(lambda e, i: e.dma_start(W2.rearrange("p k o -> p (k o)"), dr["PW"][1]))
            T.dma(lambda e, i: e.dma_start(g["brow"][0:1, 0, :], dr["PB"]))
            T.turn("tensor", lambda e, i: e.matmul(ps, g["ones"][0:1, :], g["brow"][0:1, 0, :], start=True, stop=True))
            T.turn("vector", lambda e, i: e.tensor_copy(BI, ps))

        def nodes(l=l, NH=NH):
            add_layer(l, dr["XS"][l - 1] if l else None)
            T.turn("vector", lambda e, i: e.bn_stats(st[:, 0:6], XT))
            T.turn("vector", lambda e, i: e.bn_aggr(st[:, 6:8], st[:, 0:6]))
            for fn in rsqrt_steps(st[:, 8:9], st[:, 7:8], st[:, 13:14], st[:, 14:15]):
                T.turn("vector", lambda e, i, fn=fn: fn(e))
            T.turn("vector", lambda e, i: e.scalar_tensor_tensor(st[:, 9:10], st[:, 6:7], -1.0, st[:, 8:9], ALU.mult, ALU.mult))
            T.turn("scalar", lambda e, i: e.activation(H, XT, ACT.Relu, bias=st[:, 9:10], scale=st[:, 8:9]))

            def tr(e, i):
                for k in range(4):
                    last = e.transpose(ps[:, k * P:(k + 1) * P], H[:, k * P:(k + 1) * P], ident)
                return last
            T.turn("tensor", tr)
            T.turn("vector", lambda e, i: e.tensor_copy(HT, ps))
            for k in range(4):
                T.dma(lambda e, i, k=k: e.dma_start(dr["HT"][k, :, at(e, i)], HT[:, k * P:(k + 1) * P]))

            def product(w, n, to):
                def mm(e, i):
                    for k in range(4):
                        last = e.matmul(ps[:, 0:n], HT[:, k * P:(k + 1) * P], w(k), start=k == 0, stop=k == 3)
                    return last
                T.turn("tensor", mm)
            product(lambda k: W[:, k, :], D, None)
            T.turn("vector", lambda e, i: e.tensor_copy(YT, ps))
            T.dma(lambda e, i: e.dma_start(dr["WH"][at(e, i), :], YT))
            if l == 0:
                product(lambda k: W2[:, k, :], D, None)
                T.turn("vector", lambda e, i: e.tensor_tensor(YT, ps, BI, ALU.add))
                T.dma(lambda e, i: e.dma_start(dr["V"][at(e, i), :], YT))
            else:
                product(lambda k: WE[:, l - 1, k, 8:8 + NH], NH, None)
                T.turn("vector", lambda e, i: e.tensor_copy(st[:, 16:16 + NH], ps[:, 0:NH]))
                T.dma(lambda e, i: e.dma_start(dr["S"][at(e, i), 0:NH], st[:, 16:16 + NH], allow_slow_non_contiguous=True))

        T.loop(NT, nodes)
        for k in range(4):
            T.dma(lambda e, i, k=k: e.dma_start(hT[:, k, :], dr["HT"][k, :, 0:N]))
        T.dma(lambda e, i: e.dma_start(WH[:, 0:NT - 1, :], dr["WH"][0:(NT - 1) * P, :].rearrange("(t p) o -> p t o", p=P)))
        T.dma(lambda e, i: e.dma_start(WH[0:N - (NT - 1) * P, NT - 1, :], dr["WH"][(NT - 1) * P:N, :]))

        for h in range(NH):
            if l:
                T.turn("vector", lambda e, i, l=l, h=h: e.tensor_copy(
                    WDB, WE[:, l - 1, :, h:h + 1].broadcast_to([P, 4, P])))
                for j in range(0, N, D):
                    n = min(D, N - j)

                    def db(e, i, j=j, n=n):
                        for k in range(4):
                            last = e.matmul(ps[:, 0:n], WDB[:, k, :], hT[:, k, j:j + n], start=k == 0, stop=k == 3)
                        return last
                    T.turn("tensor", db)
                    T.turn("vector", lambda e, i, j=j, n=n: e.tensor_copy(DB[:, j:j + n], ps[:, 0:n]))

            def rows(l=l, h=h, F=F):
                T.dma(lambda e, i: e.dma_start(ADJ, dr["adj"][at(e, i), :]))
                if l == 0:
                    T.turn("vector", lambda e, i: e.tensor_scalar(U, ADJ, 0.0, None, ALU.is_gt))
                    T.turn("vector", lambda e, i: e.tensor_reduce(st[:, 10:11], U, AX.X, ALU.add))
                    T.turn("vector", lambda e, i: e.tensor_scalar(st[:, 10:11], st[:, 10:11], 1.0, None, ALU.max))
                else:
                    T.dma(lambda e, i: e.dma_start(st[:, 15:16], dr["S"][at(e, i), h:h + 1], allow_slow_non_contiguous=True))
                    T.turn("vector", lambda e, i: e.tensor_scalar(U, DB, st[:, 15:16], None, ALU.add))
                    T.turn("vector", lambda e, i: e.scalar_tensor_tensor(U, U, 0.2, U, ALU.mult, ALU.max))
                    if l < 3:
                        T.turn("vector", lambda e, i: e.scalar_tensor_tensor(U, ADJ, 0.0, U, ALU.is_gt, ALU.mult))
                        T.turn("vector", lambda e, i: e.tensor_scalar(V, ADJ, 0.0, NEG, ALU.is_le, ALU.mult))
                    else:
                        T.turn("vector", lambda e, i: e.scalar_tensor_tensor(U, ADJ, 0.0, U, ALU.not_equal, ALU.mult))
                        T.turn("vector", lambda e, i: e.tensor_scalar(V, ADJ, 0.0, NEG, ALU.is_equal, ALU.mult))
                    T.turn("vector", lambda e, i: e.tensor_tensor(U, U, V, ALU.add))
                    T.turn("vector", lambda e, i: e.tensor_reduce(st[:, 11:12], U, AX.X, ALU.max))
                    T.turn("vector", lambda e, i: e.tensor_scalar(st[:, 11:12], st[:, 11:12], -1.0, None, ALU.mult))
                    T.turn("scalar", lambda e, i: e.activation(U, U, ACT.Exp, bias=st[:, 11:12], accum_out=st[:, 10:11]))
                T.turn("vector", lambda e, i: e.reciprocal(st[:, 12:13], st[:, 10:11]))
                for c in range(0, NT, 4):
                    js = [(j, min(P, N - j * P)) for j in range(c, min(c + 4, NT))]

                    def tr(e, i, js=js, c=c):
                        for j, n in js:
                            last = e.transpose(ps[0:n, (j - c) * P:(j - c + 1) * P], U[:, j * P:j * P + n], ident)
                        return last
                    T.turn("tensor", tr)
                    full = [j for j, n in js if n == P]
                    T.turn("vector", lambda e, i, c=c, m=len(full): e.tensor_copy(
                        PT[:, c:c + m, :], ps[:, 0:m * P].rearrange("p (t i) -> p t i", i=P)))
                    for j, n in js[len(full):]:
                        T.turn("vector", lambda e, i, j=j, n=n, c=c: e.tensor_copy(
                            PT[0:n, j, :], ps[0:n, (j - c) * P:(j - c + 1) * P]))

                def mm(e, i):
                    for j in range(NT):
                        n = min(P, N - j * P)
                        last = e.matmul(ps2[:, 0:F], PT[0:n, j, :], WH[0:n, j, h * F:(h + 1) * F],
                                        start=j == 0, stop=j == NT - 1)
                    return last
                T.turn("tensor", mm)
                T.turn("vector", lambda e, i: e.tensor_scalar(V[:, 0:F], ps2[:, 0:F], st[:, 12:13], None, ALU.mult))
                T.dma(lambda e, i: e.dma_start(dr["Y"][at(e, i), h * F:(h + 1) * F], V[:, 0:F]))

            T.loop(NT, rows)
    T.loop(NT, lambda: add_layer(4, dr["out"]))


BF16 = mybir.dt.bfloat16
FP16 = mybir.dt.float16
U32 = mybir.dt.uint32
NC = 5
NK = 16
SEG = 416
NSEG = 8
ROW = 520
FAR = 4096.0


class Queues:

    def __init__(self, nc, ctx):
        self.nc, self.ctx = nc, ctx
        self.sem = {e: ctx.enter_context(nc.semaphore(f"q_{e}")) for e in ENGINES[1:]}
        self.count = dict.fromkeys(self.sem, 0)
        self.slots = {}
        self.marks = {}
        self.items = {e: [] for e in ENGINES}

    def op(self, engine, fn, key=None):
        if key is not None:
            self.count[engine] += 1
            assert key not in self.marks, key
            self.marks[key] = (self.sem[engine], self.count[engine])
        self.items[engine].append((fn, self.sem[engine] if key is not None else None, 1))

    def dma(self, engine, fn, slot, key):
        if slot not in self.slots:
            self.slots[slot] = [self.ctx.enter_context(self.nc.semaphore(f"d_{slot}")), 0]
        s = self.slots[slot]
        s[1] += 16
        self.marks[key] = (s[0], s[1])
        self.items[engine].append((fn, s[0], 16))

    def wait(self, engine, *keys):
        for key in keys:
            self.items[engine].append((None, key, 0))

    def emit(self, e, name):
        met = {}
        for fn, x, n in self.items[name]:
            if fn is None:
                sem, value = self.marks[x]
                if met.get(id(sem), 0) < value:
                    met[id(sem)] = value
                    e.wait_ge(sem, value)
            else:
                last = fn(e)
                if x is not None:
                    last.then_inc(x, n)


def sparse(Q, nc, g, dr):
    f, psum = g["f"], g["psum"]
    ident, WE = g["ident"], g["WE"]
    V, S, T, G, SP = "vector", "scalar", "tensor", "gpsimd", "sync"

    at = [0]

    def take(n, shape=None, dt=None):
        v = f(at[0], n)
        at[0] += n
        if dt is not None:
            v = v.bitcast(dt)
        return v if shape is None else v.rearrange(shape[0], **shape[1])

    X = take(NT * D, ("p (t o) -> p t o", dict(o=D)))
    Sb = take(NT * 320, ("p (t c i) -> p t c i", dict(c=NC, i=P)), BF16)
    STb = take(NT * 320, ("p (t e) -> p t e", dict(t=NT)), BF16)
    WL = [take(4 * D, ("p (k o) -> p k o", dict(k=4))) for _ in range(2)]
    K1 = take(NT * 40, ("p (t c k) -> p t c k", dict(c=NC, k=NK)), BF16)
    IDX = take(NT * 6, ("p (t c) -> p t c", dict(c=6)), U32)
    SM = take(2 * NT * 16, ("p (a t h) -> p a t h", dict(a=2, h=16)))
    R = take(NT * 18, ("p (t c) -> p t c", dict(c=18)))
    NEGM = take(NT * NK, ("p (t k) -> p t k", dict(k=NK)))
    DEG, END, FL, RDEG, HS = take(NT), take(NT), take(NT), take(NT), take(4 * NT, ("p (k t) -> p k t", dict(k=4)))
    UPPER = take(P)
    I128, K16, EC, ROWID = take(P), take(NK), take(NC), take(1)
    hsum, mrow = take(4), take(ROW)
    small = take(64)
    H = take(D)
    HT = take(D, ("p (k i) -> p k i", dict(k=4)))
    WO = [take(ROW) for _ in range(2)]
    shared = at[0]
    ADJ = [take(N + 1) for _ in range(2)]
    HALF = NSEG * SEG // 2
    IO = take(HALF // 2, None, FP16)
    MARK = take(HALF, None, FP16)
    CAND, CAND2 = take(64), take(64)
    VO = take(D)
    tmp16 = take(NK)
    kk, colf, z5 = take(NC), take(NC), take(NC)
    tmp80 = take(NC * NK, ("p (c k) -> p c k", dict(c=NC)))
    E640, A640, STF = take(640), take(320, None, FP16), take(640)
    assert at[0] <= g["arena_words"], at[0]
    at[0] = shared
    GB = [take(NC * ROW, ("p (c o) -> p c o", dict(c=NC))) for _ in range(2)]
    PG = [take(D) for _ in range(3)]
    S2 = [take(640, ("p (c i) -> p c i", dict(c=NC))) for _ in range(2)]
    ST32 = take(640)
    DK = take(NC * NK * 8)
    EM = take(NK * 8)
    U5 = take(NC * 8, ("p (c h) -> p c h", dict(c=NC)))
    P2 = [take(NC * 8, ("p (c h) -> p c h", dict(c=NC))) for _ in range(2)]
    Y = take(D)
    VT = [take(D) for _ in range(2)]
    Y2 = VT[0]
    rden, u8 = take(8), take(8)
    end2 = at[0]
    assert end2 <= g["arena_words"], end2

    p_ell, p_q, p_t, p_den, p_small = psum[:, 0, :], psum[:, 1, :], psum[:, 4, :], psum[:, 7, :], psum[:, 7, :]
    p_num = [psum[:, 2, :], psum[:, 3, :]]
    p_wh = psum[:, 5:7, :].rearrange("p b o -> p (b o)")

    def rows(t):
        return min(P, N - t * P)

    def parts(t):
        return [(0, P)] if t < NT - 1 else [(0, 112), (112, rows(t))]

    def vec(fn, *after, key=None, dep=True):
        if dep and vec.n:
            Q.wait(V, ("v", vec.n - 1))
        Q.wait(V, *after)
        Q.op(V, fn, ("v", vec.n))
        if key is not None:
            Q.marks[key] = Q.marks["v", vec.n]
        vec.n += 1
    vec.n = 0

    def pool(fn, key, *after):
        if pool.last:
            Q.wait(G, pool.last)
        Q.wait(G, *after)
        Q.op(G, fn, key)
        pool.last = key
    pool.last = None
    const = pool
    const(lambda e: e.iota(IO, pattern=[[1, HALF]], base=1, channel_multiplier=0,
                           allow_small_or_imprecise_dtypes=True), "iota")
    const(lambda e: e.memset(MARK, 0.0), "mark0")
    const(lambda e: e.iota(E640, pattern=[[1, 640]], base=0, channel_multiplier=0,
                           allow_small_or_imprecise_dtypes=True), "e640")
    const(lambda e: e.iota(I128, pattern=[[1, P]], base=1, channel_multiplier=0,
                           allow_small_or_imprecise_dtypes=True), "i128")
    const(lambda e: e.iota(K16, pattern=[[1, NK]], base=0, channel_multiplier=0,
                           allow_small_or_imprecise_dtypes=True), "k16")
    const(lambda e: e.iota(EC, pattern=[[P, NC]], base=0, channel_multiplier=1,
                           allow_small_or_imprecise_dtypes=True), "ec")
    const(lambda e: e.iota(ROWID, pattern=[[0, 1]], base=1, channel_multiplier=1,
                           allow_small_or_imprecise_dtypes=True), "rowid")
    const(lambda e: e.memset(UPPER, 1.0), "upper0")
    const(lambda e: e.affine_select(out=UPPER, in_=UPPER, compare_op=ALU.is_gt, fill=0.0, base=0,
                                    pattern=[[1, P]], channel_multiplier=-1), "upper")
    const(lambda e: e.memset(mrow, 0.0), "mrow0")
    const(lambda e: e.memset(SM.rearrange("p a t h -> p (a t h)"), 0.0), "sm0")
    const(lambda e: e.memset(X[96:P, NT - 1, :], 0.0), "xpad")

    def load(dst, src, t, slot, key, engine=SP):
        for n, (a, b) in enumerate(parts(t)):
            Q.dma(engine, lambda e, a=a, b=b: e.dma_start(dst[a:b, :], src[t * P + a:t * P + b, :]),
                  f"{slot}_{n}" if n else slot, (key, n))
        return [(key, n) for n in range(len(parts(t)))]

    def adj_tile(t):
        if t >= 2:
            Q.wait(SP, ("mark", t - 2))
        if t == NT - 1:
            Q.wait(SP, "adjpad")
        return load(ADJ[t % 2].bitcast(I32)[:, 0:N], dr["adj"], t, f"adj{t % 2}", ("adj", t))

    def weights(l, key):
        at_, which = {0: (0, 0), 10: (1, 1), 1: (0, 2), 2: (1, 3), 3: (0, 4)}[l]
        Q.dma(SP, lambda e: e.dma_start(WL[at_].rearrange("p k o -> p (k o)"), dr["PW"][which]), f"wl{at_}", key)

    adj_keys, x_keys = {}, {}
    adj_keys[0] = adj_tile(0)
    weights(0, ("w", 0))
    weights(10, ("w", 10))
    Q.wait(SP, "xpad", "mrow0")
    Q.dma(SP, lambda e: e.dma_start(dr["T"][0][N:N + 1, :], mrow[0:1, 0:D]), "zero", "zero")
    Q.dma(SP, lambda e: e.dma_start(g["brow"][0:1, 0, :], dr["PB"]), "bias", "bias")
    for t in range(NT):
        x_keys[t] = load(X[:, t, :], dr["x"], t, f"x{t % 4}", ("x", t)) if t < 4 else None
    for t in range(1, 2):
        adj_keys[t] = adj_tile(t)

    def layernorm(t, x, after):
        n = rows(t)
        st = small[0:n, :]
        vec(lambda e: e.bn_stats(st[:, 0:6], x[0:n, :]), *after)
        vec(lambda e: e.bn_aggr(st[:, 6:8], st[:, 0:6]))
        if ("h", layernorm.n - 1) in Q.marks:
            Q.wait(V, ("h", layernorm.n - 1))
        for fn in rsqrt_steps(st[:, 8:9], st[:, 7:8], st[:, 13:14], st[:, 14:15]):
            vec(fn)
        vec(lambda e: e.scalar_tensor_tensor(st[:, 9:10], st[:, 6:7], -1.0, st[:, 8:9], ALU.mult, ALU.mult),
            key=("ln", layernorm.n))

    layernorm.n = 0

    def node_h(t, x, m):
        n = rows(t)
        Q.wait(S, ("ln", m))
        if m:
            Q.wait(S, ("tr", m - 1))
        Q.op(S, lambda e: e.activation(H[0:n, :], x[0:n, :], ACT.Relu, bias=small[0:n, 9:10], scale=small[0:n, 8:9]),
             ("h", m))

    def node_tr(t, m):
        n = rows(t)
        Q.wait(T, ("h", m))
        if m:
            Q.wait(T, ("ht", m - 1))
        for k in range(4):
            Q.op(T, lambda e, k=k: e.transpose(p_t[:, k * P:k * P + n], H[0:n, k * P:(k + 1) * P], ident[0:n, 0:n]),
                 ("tr", m) if k == 3 else None)

    def node_ht(t, m, sums):
        n = rows(t)
        Q.wait(S, ("tr", m))
        if m:
            Q.wait(S, ("proj", m - 1))
        if sums:
            for k in range(4):
                Q.op(S, lambda e, k=k: e.activation(HT[:, k, 0:n], p_t[:, k * P:k * P + n], ACT.Copy,
                                                    accum_out=HS[:, k, t:t + 1]), ("ht", m) if k == 3 else None)
        else:
            Q.op(S, lambda e: e.activation(HT[:, :, 0:n], p_t.rearrange("p (k i) -> p k i", k=4)[:, :, 0:n], ACT.Copy),
                 ("ht", m))

    def marks(t):
        Q.wait(S, *adj_keys[t], "mark0")
        if t:
            Q.wait(S, ("scan", t - 1))
        Q.op(S, lambda e: e.activation(MARK[:, 0:N], ADJ[t % 2].bitcast(I32)[:, 0:N], ACT.Sign), ("mark", t))

    def scan(t):
        if t == NT - 3:
            Q.wait(G, ("mark", t))
            pool(lambda e: e.memset(ADJ[(NT - 1) % 2][96:P, :], 0.0), "adjpad")
        vec(lambda e: e.tensor_tensor(MARK.rearrange("p (a n) -> p a n", a=2), MARK.rearrange("p (a n) -> p a n", a=2),
                                      IO.unsqueeze(1).broadcast_to([P, 2, HALF]), ALU.mult), ("mark", t), "iota")
        for s in range(NSEG):
            vec(lambda e, s=s: e.max(CAND[:, s * 8:s * 8 + 8], MARK[:, s * SEG:(s + 1) * SEG]), dep=s == 0,
                key=("scan", t) if s == NSEG - 1 else None)
        if t + 1 < NT:
            marks(t + 1)
        vec(lambda e: e.tensor_scalar(CAND2[:, 32:64], CAND[:, 32:64], 0.0, float(HALF), ALU.is_gt, ALU.mult))
        vec(lambda e: e.tensor_tensor(CAND[:, 32:64], CAND[:, 32:64], CAND2[:, 32:64], ALU.add))
        r = R[:, t, :]
        vec(lambda e: e.max(r[:, 0:8], CAND))
        vec(lambda e: e.tensor_reduce(FL[:, t:t + 1], CAND.rearrange("p (s k) -> p s k", k=8)[:, :, 7], AX.X, ALU.max), dep=False)
        vec(lambda e: e.match_replace(CAND2, r[:, 0:8], CAND, 0.0))
        vec(lambda e: e.max(r[:, 8:16], CAND2))
        vec(lambda e: e.tensor_scalar(tmp16, r[:, 0:16], 0.0, 0.0, ALU.is_gt, ALU.add, accum_out=DEG[:, t:t + 1]))
        vec(lambda e: e.tensor_scalar(tmp16[:, 0:1], DEG[:, t:t + 1], 0.0, float(N + 1), ALU.is_equal, ALU.mult))
        vec(lambda e: e.tensor_tensor(r[:, 0:1], r[:, 0:1], tmp16[:, 0:1], ALU.add))
        vec(lambda e: e.tensor_scalar(DEG[:, t:t + 1], DEG[:, t:t + 1], 1.0, None, ALU.max), dep=False, key=("deg", t))
        vec(lambda e: e.tensor_copy(r[:, 17:18], ROWID), "rowid", dep=False)
        vec(lambda e: e.tensor_scalar(NEGM[:, t, :], K16, DEG[:, t:t + 1], -1e30, ALU.is_ge, ALU.mult), "k16")
        Q.wait(T, ("deg", t), "upper")
        if t:
            Q.wait(T, ("end", t - 1))
        Q.op(T, lambda e: e.matmul(p_small[:, 0:1], UPPER, DEG[:, t:t + 1], start=True, stop=True), ("off", t))

    def lists(t):
        r = R[:, t, :]
        vec(lambda e: e.tensor_copy(r[:, 16:17], p_small[:, 0:1]), ("off", t))
        vec(lambda e: e.tensor_tensor(END[:, t:t + 1], DEG[:, t:t + 1], p_small[:, 0:1], ALU.add), key=("end", t), dep=False)
        vec(lambda e: e.tensor_scalar(A640, E640, r[:, 16:17], None, ALU.is_ge), "e640")
        vec(lambda e: e.scalar_tensor_tensor(STF, E640, END[:, t:t + 1], A640, ALU.is_lt, ALU.mult),
            *([("stb", t - 1), ("edges", t - 1)] if t else []), key=("stf", t))
        Q.wait(S, ("stf", t))
        Q.op(S, lambda e: e.activation(STb[:, t, :], STF, ACT.Copy), ("stb", t))
        Q.wait(T, ("stf", t))
        if t:
            Q.wait(T, ("sb", t - 1))
        for c in range(NC):
            Q.op(T, lambda e, c=c: e.matmul(p_q[:, c * 18:(c + 1) * 18], STF[:, c * P:(c + 1) * P], r, start=True, stop=True),
                 ("edges", t) if c == NC - 1 else None)
        pe = p_q[:, 0:NC * 18].rearrange("p (c k) -> p c k", k=18)
        vec(lambda e: e.tensor_tensor(kk, EC, pe[:, :, 16], ALU.subtract), ("edges", t), "ec")
        vec(lambda e: e.tensor_tensor(K1[:, t, :, :], K16.unsqueeze(1).broadcast_to([P, NC, NK]),
                                      kk.unsqueeze(2).broadcast_to([P, NC, NK]), ALU.is_equal))
        vec(lambda e: e.tensor_tensor(tmp80, K1[:, t, :, :], pe[:, :, 0:NK], ALU.mult))
        vec(lambda e: e.tensor_reduce(colf, tmp80, AX.X, ALU.add))
        vec(lambda e: e.tensor_scalar(z5, colf, 0.0, FAR, ALU.is_equal, ALU.mult))
        vec(lambda e: e.scalar_tensor_tensor(IDX[:, t, 0:NC], colf, -1.0, z5, ALU.add, ALU.add), key=("idx", t))
        vec(lambda e: e.tensor_tensor(Sb[:, t, :, :], I128.unsqueeze(1).broadcast_to([P, NC, P]),
                                      pe[:, :, 17:18].broadcast_to([P, NC, P]), ALU.is_equal), "i128", key=("sb", t))

    def own(t):
        n = rows(t)
        node_tr(t, t)
        node_ht(t, t, False)
        def one(which, key):
            Q.wait(T, ("ht", t), ("w", 10 * which), "bias")
            if t:
                Q.wait(T, ("wo", t - 1) if which == 0 else ("vo", t - 1))
            dst = p_num[which]
            for k in range(4):
                Q.op(T, lambda e, k=k: e.matmul(dst[0:n, :], HT[:, k, 0:n], WL[which][:, k, :], start=k == 0,
                                                stop=k == 3 and which == 0), (key, t) if k == 3 and which == 0 else None)
            if which:
                Q.op(T, lambda e: e.matmul(dst[0:n, :], g["ones"][0:1, 0:n], g["brow"][0:1, 0, :], start=False, stop=True), (key, t))
                Q.marks["proj", t] = Q.marks[key, t]
            buf = VO if which else WO[0]
            Q.wait(S, (key, t))
            if t:
                Q.wait(S, *[("vout" if which else "tout", 0, t - 1, q) for q in range(len(parts(t - 1)))])
            Q.op(S, lambda e: e.activation(buf[0:n, 0:D], dst[0:n, :], ACT.Copy), ("vo" if which else "wo", t))
            Q.wait(SP, ("vo" if which else "wo", t))
            for q, (a, b) in enumerate(parts(t)):
                Q.dma(SP, lambda e, a=a, b=b: e.dma_start((dr["V"] if which else dr["T"][0])[t * P + a:t * P + b, :], buf[a:b, 0:D]),
                      f"{'vout' if which else 'tout'}{q}", ("vout" if which else "tout", 0, t, q))

        one(0, "pa")
        one(1, "pb")

    marks(0)
    for t in range(NT):
        scan(t)
        if t + 2 < NT:
            adj_keys[t + 2] = adj_tile(t + 2)
        layernorm.n = t
        for nt in (t + 1, t + 2, t + 3):
            if nt < NT and nt >= 4 and x_keys.get(nt) is None:
                x_keys[nt] = load(X[:, nt, :], dr["x"], nt, f"x{nt % 4}", ("x", nt))
        layernorm(t, X[:, t, :], x_keys[t])
        lists(t)
        node_h(t, X[:, t, :], t)
        own(t)

    fl = small[:, 32:36]
    vec(lambda e: e.tensor_reduce(fl[:, 0:1], FL, AX.X, ALU.max))
    vec(lambda e: e.tensor_reduce(fl[:, 1:2], R[:, :, 15], AX.X, ALU.max), dep=False)
    vec(lambda e: e.tensor_reduce(fl[:, 2:3], END, AX.X, ALU.max), dep=False)
    vec(lambda e: e.tensor_scalar(fl[:, 2:3], fl[:, 2:3], float(NC * P), None, ALU.is_gt))
    vec(lambda e: e.tensor_reduce(fl[:, 3:4], fl[:, 0:3], AX.X, ALU.max))
    vec(lambda e: e.reciprocal(RDEG, DEG), key="rdeg")
    Q.wait(T, "rdeg", ("end", NT - 1))
    Q.op(T, lambda e: e.matmul(p_small[:, 0:1], g["ones"], fl[:, 3:4], start=True, stop=True), "flag0")
    vec(lambda e: e.tensor_scalar(g["flag"], p_small[:, 0:1], 0.5, None, ALU.is_gt), "flag0", key="flag")

    Q.wait(G, "flag", ("stb", NT - 1), ("vo", NT - 1))
    Q.wait(G, *[("vout", 0, NT - 1, q) for q in range(2)])
    for s in range(2):
        pool(lambda e, s=s: e.memset(GB[s].rearrange("p c o -> p (c o)"), 0.0), ("g0", s))

    for l in range(4):
        NH, F = HEADS[l], D // HEADS[l]
        width = ROW if l else D
        par = l % 2
        if l < 3:
            if l == 0:
                Q.wait(SP, ("proj", NT - 1))
            else:
                Q.wait(SP, ("mean", l - 1) if l >= 2 else ("proj", NT - 1))
            weights(l + 1, ("w", l + 1))
        tkeys = [("tout", l, t, q) for t in range(NT) for q in range(len(parts(t)))]

        def gather(t, l=l, width=width, tkeys=tkeys):
            s = t % 2
            i = l * NT + t
            if t == 0:
                Q.wait(G, *tkeys, ("meanout", l) if l else "zero", ("g0", 0), ("g0", 1))
            Q.wait(G, ("idx", t))
            if i >= 2:
                Q.wait(G, ("pg", i - 2))
            for c in range(NC):
                Q.dma(G, lambda e, c=c: e.indirect_dma_start(
                    GB[s][:, c, 0:width], None, dr["T"][l],
                    bass.IndirectOffsetOnAxis(ap=IDX[:, t, c:c + 1], axis=0), bounds_check=N, oob_is_err=False),
                    f"g{s}{c}", ("g", i, c))

        def alpha(t, l=l, NH=NH, par=par):
            i, s = l * NT + t, t % 2
            S32, PE5 = S2[i % 2], P2[i % 2]
            if i >= 2:
                Q.wait(S, ("num", i - 2))
            if i == 0:
                Q.wait(S, ("g0", 1))
            Q.op(S, lambda e: e.activation(S32.rearrange("p c i -> p (c i)"), Sb[:, t, :, :].rearrange("p c i -> p (c i)"),
                                           ACT.Copy), ("s32", i))
            if l == 0:
                return
            if i > NT:
                Q.wait(S, ("sme", i - 1))
            Q.op(S, lambda e: e.activation(ST32, STb[:, t, :], ACT.Copy), ("st32", i))
            d = GB[s][:, :, D:D + NH]
            dk = DK[:, 0:NC * NK * NH].rearrange("p (c k h) -> p c k h", c=NC, k=NK)
            vec(lambda e: e.tensor_tensor(dk, K1[:, t, :, :].unsqueeze(3).broadcast_to([P, NC, NK, NH]),
                                          d.unsqueeze(2).broadcast_to([P, NC, NK, NH]), ALU.mult),
                *[("g", i, c) for c in range(NC)], key=("dk", i))
            Q.wait(T, ("dk", i), ("s32", i))
            for c in range(NC):
                Q.op(T, lambda e, c=c: e.matmul(p_ell[:, 0:NK * NH], S32[:, c, :], DK[:, c * NK * NH:(c + 1) * NK * NH],
                                                start=c == 0, stop=c == NC - 1), ("ell", i) if c == NC - 1 else None)
            em = EM[:, 0:NK * NH].rearrange("p (k h) -> p k h", k=NK)
            vec(lambda e: e.tensor_tensor(em, p_ell[:, 0:NK * NH].rearrange("p (k h) -> p k h", k=NK),
                                          NEGM[:, t, :].unsqueeze(2).broadcast_to([P, NK, NH]), ALU.add), ("ell", i))
            vec(lambda e: e.tensor_reduce(u8[:, 0:NH], EM[:, 0:NK * NH].rearrange("p (k h) -> p h k", k=NK), AX.X, ALU.max))
            sm = SM[:, par, t, :]
            vec(lambda e: e.tensor_tensor(u8[:, 0:NH], u8[:, 0:NH], sm[:, 0:NH], ALU.add), ("sm", l, t), "sm0")
            vec(lambda e: e.scalar_tensor_tensor(sm[:, 8:8 + NH], u8[:, 0:NH], 0.2, u8[:, 0:NH], ALU.mult, ALU.max), key=("m8", i))
            Q.wait(T, ("m8", i), ("st32", i))
            for c in range(NC):
                Q.op(T, lambda e, c=c: e.matmul(p_q[:, c * 16:(c + 1) * 16], ST32[:, c * P:(c + 1) * P], sm, start=True, stop=True),
                     ("sme", i) if c == NC - 1 else None)
            pq = p_q[:, 0:NC * 16].rearrange("p (c h) -> p c h", h=16)
            if i - 1 >= NT:
                Q.wait(V, ("exp", i - 1))
            vec(lambda e: e.tensor_tensor(U5[:, :, 0:NH], d, pq[:, :, 0:NH], ALU.add), ("sme", i))
            vec(lambda e: e.scalar_tensor_tensor(U5[:, :, 0:NH], U5[:, :, 0:NH], 0.2, U5[:, :, 0:NH], ALU.mult, ALU.max))
            vec(lambda e: e.tensor_tensor(U5[:, :, 0:NH], U5[:, :, 0:NH], pq[:, :, 8:8 + NH], ALU.subtract), key=("u5", i))
            Q.wait(S, ("u5", i))
            Q.op(S, lambda e: e.activation(PE5[:, :, 0:NH], U5[:, :, 0:NH], ACT.Exp), ("exp", i))

        def beta(t, l=l, NH=NH, F=F):
            i, s = l * NT + t, t % 2
            num, S32, PE5 = p_num[i % 2], S2[i % 2], P2[i % 2]
            if l:
                vec(lambda e: e.tensor_scalar(PE5[:, :, 0:NH], PE5[:, :, 0:NH], 1.0, None, ALU.min), ("exp", i), key=("p", i))
            if i >= 2:
                Q.wait(T, ("y", i - 2))
            for c in range(NC):
                j = i * NC + c
                if l:
                    vec(lambda e, c=c, j=j: e.tensor_tensor(
                        PG[j % 3].rearrange("p (h o) -> p h o", h=NH), GB[s][:, c, 0:D].rearrange("p (h o) -> p h o", h=NH),
                        PE5[:, c, 0:NH].unsqueeze(2).broadcast_to([P, NH, F]), ALU.mult),
                        ("g", i, c), *([("used", j - 3)] if ("used", j - 3) in Q.marks else []), key=("pgc", j), dep=c == 0)
                    Q.wait(T, ("pgc", j), ("s32", i))
                    rhs = PG[j % 3]
                else:
                    Q.wait(T, ("g", i, c), ("s32", i))
                    rhs = GB[s][:, c, 0:D]
                Q.op(T, lambda e, c=c, rhs=rhs: e.matmul(num, S32[:, c, :], rhs, start=c == 0, stop=c == NC - 1), ("used", j))
            if l:
                Q.marks["pg", i] = Q.marks["pgc", i * NC + NC - 1]
                if i > NT:
                    Q.wait(T, ("rden", i - 1))
                for c in range(NC):
                    Q.op(T, lambda e, c=c: e.matmul(p_den[:, 0:NH], S32[:, c, :], PE5[:, c, 0:NH], start=c == 0, stop=c == NC - 1),
                         ("num", i) if c == NC - 1 else None)
            else:
                Q.marks["num", i] = Q.marks["pg", i] = Q.marks["used", i * NC + NC - 1]

        def gamma(t, l=l, NH=NH, F=F):
            i = l * NT + t
            n = rows(t)
            num = p_num[i % 2]
            x = X[:, t, :]
            if l == 0:
                vec(lambda e: e.scalar_tensor_tensor(Y, num, RDEG[:, t:t + 1], VT[t % 2], ALU.mult, ALU.add),
                    ("num", i), *[("v", "in", t, q) for q in range(len(parts(t)))], key=("y", i))
                vec(lambda e: e.scalar_tensor_tensor(x, Y, 0.0, x, ALU.max, ALU.add))
            else:
                vec(lambda e: e.reciprocal(rden[:, 0:NH], p_den[:, 0:NH]), ("num", i), key=("rden", i))
                if l == 3:
                    if t >= 2:
                        Q.wait(V, *[("out", t - 2, q) for q in range(len(parts(t - 2)))])
                    out = VT[t % 2]
                    vec(lambda e: e.scalar_tensor_tensor(out, num, rden[:, 0:1], x, ALU.mult, ALU.add), key=("y", i))
                    Q.wait(SP, ("y", i))
                    for q, (a, b) in enumerate(parts(t)):
                        Q.dma(SP, lambda e, a=a, b=b: e.dma_start(dr["out"][t * P + a:t * P + b, :], out[a:b, :]),
                              f"out{t % 2}{q}", ("out", t, q))
                    return
                vec(lambda e: e.tensor_tensor(Y.rearrange("p (h o) -> p h o", h=NH), num.rearrange("p (h o) -> p h o", h=NH),
                                              rden[:, 0:NH].unsqueeze(2).broadcast_to([P, NH, F]), ALU.mult), key=("y", i))
                if l == 2:
                    vec(lambda e: e.tensor_scalar(Y2, Y, 0.0, None, ALU.min), key=("mn", i))
                    Q.wait(S, ("mn", i))
                    Q.op(S, lambda e: e.activation(Y2, Y2, ACT.Exp), ("elu", i))
                    vec(lambda e: e.scalar_tensor_tensor(Y, Y, 0.0, x, ALU.max, ALU.add))
                    vec(lambda e: e.scalar_tensor_tensor(x, Y2, -1.0, Y, ALU.add, ALU.add), ("elu", i))
                else:
                    vec(lambda e: e.tensor_tensor(x, x, Y, ALU.add))
            m = (l + 1) * NT + t
            layernorm.n = m
            layernorm(t, x, [])
            node_h(t, x, m)

        def delta(t, l=l):
            if l == 3:
                return
            n = rows(t)
            m = (l + 1) * NT + t
            w = WL[l % 2]
            node_tr(t, m)
            node_ht(t, m, True)
            Q.wait(T, ("ht", m), ("w", l + 1), ("wo", m - 1))
            for k in range(4):
                Q.op(T, lambda e, k=k: e.matmul(p_wh[0:n, 0:D], HT[:, k, 0:n], w[:, k, :], start=k == 0, stop=k == 3))
            for k in range(4):
                Q.op(T, lambda e, k=k: e.matmul(p_wh[0:n, D:D + 16], HT[:, k, 0:n], WE[:, l, k, :], start=k == 0, stop=k == 3),
                     ("proj", m) if k == 3 else None)
            buf = WO[t % 2]
            Q.wait(S, ("proj", m))
            key = lambda q, tt: ("tout", l + 1, tt, q)
            if t >= 2:
                Q.wait(S, *[key(q, t - 2) for q in range(len(parts(t - 2)))])
            elif l:
                Q.wait(S, *[("tout", l, tt, q) for tt in (NT - 2, NT - 1) for q in range(len(parts(tt)))])
            else:
                Q.wait(S, *[("tout", 0, NT - 1, q) for q in range(2)])
            Q.op(S, lambda e: e.activation(buf[0:n, :], p_wh[0:n, 0:ROW], ACT.Copy), ("wo1", m))
            Q.op(S, lambda e: e.activation(SM[0:n, (l + 1) % 2, t, 0:8], p_wh[0:n, ROW:ROW + 8], ACT.Copy), ("wo", m))
            Q.marks["sm", l + 1, t] = Q.marks["wo", m]
            Q.wait(SP, ("wo1", m))
            for q, (a, b) in enumerate(parts(t)):
                Q.dma(SP, lambda e, a=a, b=b: e.dma_start(dr["T"][l + 1][t * P + a:t * P + b, :], buf[a:b, :]),
                      f"to{t % 2}{q}", key(q, t))

        def vload(t):
            if l == 0 and t < NT:
                if t >= 2:
                    Q.wait(SP, ("y", t - 2))
                else:
                    Q.wait(SP, ("g0", 1), *[("vout", 0, tt, q) for tt in range(NT) for q in range(len(parts(tt)))])
                for q, (a, b) in enumerate(parts(t)):
                    Q.dma(SP, lambda e, a=a, b=b: e.dma_start(VT[t % 2][a:b, :], dr["V"][t * P + a:t * P + b, :]),
                          f"v{t % 2}{q}", ("v", "in", t, q))

        if l == 0:
            pool(lambda e: e.memset(VT[(NT - 1) % 2][96:P, :], 0.0), "vpad")
            Q.wait(SP, "vpad")
            vload(0)
            vload(1)
        gather(0)
        gather(1)
        for t in range(NT + 2):
            if t < NT:
                alpha(t)
            if 2 <= t:
                delta(t - 2)
            if 1 <= t <= NT:
                beta(t - 1)
                gamma(t - 1)
                vload(t + 1)
                if t + 1 < NT:
                    gather(t + 1)
        if l < 3:
            m = (l + 1) * NT + NT - 1
            vec(lambda e: e.tensor_reduce(hsum, HS, AX.X, ALU.add), ("ht", m))
            vec(lambda e: e.tensor_scalar(hsum, hsum, 1.0 / N, None, ALU.mult), key=("hsum", l))
            Q.wait(T, ("hsum", l), ("ht", m))
            for k in range(4):
                Q.op(T, lambda e, k=k, l=l: e.matmul(p_t[0:1, :], hsum[:, k:k + 1], WL[l % 2][:, k, :], start=k == 0, stop=k == 3),
                     ("mean", l) if k == 3 else None)
            Q.wait(S, ("mean", l))
            if l:
                Q.wait(S, ("meanout", l))
            Q.op(S, lambda e: e.activation(mrow[0:1, 0:D], p_t[0:1, :], ACT.Copy), ("mrow", l))
            Q.wait(T, ("mrow", l))
            Q.wait(SP, ("mrow", l), "zero")
            Q.dma(SP, lambda e, l=l: e.dma_start(dr["T"][l + 1][N:N + 1, :], mrow[0:1, :]), "meanout", ("meanout", l + 1))
    Q.wait(SP, *[("out", t, q) for t in (NT - 2, NT - 1) for q in range(len(parts(t)))])


_W = {"W_self": "L0_gnn_W_self", "b_self": "L0_gnn_b_self", "W_nb": "L0_gnn_W_nb", "b_nb": "L0_gnn_b_nb",
      "W_comb": "L0_gnn_W_comb", "b_comb": "L0_gnn_b_comb", "W1": "L1_gnn_W", "a1": "L1_gnn_a",
      "W2": "L2_gnn_W", "a2": "L2_gnn_a", "W3": "L3_gnn_W", "a30": "L3_gnn_a1", "a31": "L3_gnn_a2"}


def program(nc, ins, out):
    dr = {k: ins[v] for k, v in _W.items()}
    dr.update(x=ins["x"], adj=ins["adj"], out=out)
    with ExitStack() as ctx:
        def scratch(name, shape):
            return nc.dram_tensor(name, shape, FP32, kind="Internal").ap()
        dr["PW"] = scratch("PW", [5, P, 4 * D])
        dr["PB"] = scratch("PB", [1, D])
        dr["XS"] = scratch("XS", [3, N, D])
        dr["Y"] = scratch("Y", [N, D])
        dr["V"] = scratch("V", [N, D])
        dr["WH"] = scratch("WH", [N, D])
        dr["HT"] = scratch("HT", [4, P, N])
        dr["S"] = scratch("S", [N, 8])
        dr["T"] = [scratch(f"T{l}", [N + 1, ROW if l else D]) for l in range(4)]
        words = 51660
        arena = ctx.enter_context(nc.sbuf_tensor("arena", [P, words], FP32))
        misc = ctx.enter_context(nc.sbuf_tensor("misc", [P, 1536], FP32))
        flag = ctx.enter_context(nc.sbuf_tensor("flag", [P, 1], I32))
        psum = ctx.enter_context(nc.psum_tensor("psum", [P, 8, D], FP32))

        def f(o, n):
            return arena[:, o:o + n]
        g = {"f": f, "arena_words": words, "ident": misc[:, 0:128], "ones": misc[:, 128:256],
             "WE": misc[:, 256:448].rearrange("p (l k h) -> p l k h", l=3, k=4),
             "bcol": misc[:, 448:452], "small": misc[:, 460:500],
             "brow": misc[:, 512:1536].rearrange("p (a n) -> p a n", a=2),
             "wa": f(0, 2048).rearrange("p (k o) -> p k o", k=4), "wb": f(2048, 2048).rearrange("p (k o) -> p k o", k=4),
             "wc": f(4096, 2048).rearrange("p (k o) -> p k o", k=4), "flag": flag[:, :], "psum": psum,
             "ps": psum[:, 0, :], "ps2": psum[:, 1, :], "ps3": psum[:, 2, :]}

        def run(name, emit):
            with nc.Block(name) as block:
                for engine, on in zip(ENGINES, (block.sync, block.tensor, block.vector, block.scalar, block.gpsimd)):
                    on(lambda e, engine=engine: emit(e, engine))

        T = Turns(nc, ctx, "prep")
        T.turn("gpsimd", lambda e, i: e.memset(g["ident"], 0.0))
        T.turn("gpsimd", lambda e, i: e.memset(g["ones"], 1.0))
        T.turn("gpsimd", lambda e, i: e.memset(misc[:, 256:448], 0.0))
        T.turn("gpsimd", lambda e, i: e.affine_select(out=g["ident"], in_=g["ident"], compare_op=ALU.not_equal,
                                                      fill=1.0, base=0, pattern=[[-1, P]], channel_multiplier=1))
        chain_prep(T, nc, g, dr)
        T.turn("sync", None)
        run("prep", T.emit)
        Q = Queues(nc, ctx)
        sparse(Q, nc, g, dr)
        run("edges", Q.emit)
        Dn = Turns(nc, ctx, "dense")
        chain_dense(Dn, nc, g, dr)

        def fallback(e, name):
            full = e.value_load(g["flag"][0:1, 0:1], min_val=0, max_val=1)
            with e.If(full.eq(1)):
                Dn.emit(e, name)
        run("dense", fallback)


_INS = ["x", "adj", *_W.values()]


def kernel(**inputs):
    import numpy as _np
    import concourse.bacc as _bacc
    from concourse import mybir as _mybir
    from concourse.bass_utils import run_bass_kernel_spmd as _run

    nc = _bacc.Bacc("TRN2", target_bir_lowering=False, num_devices=1)
    arrays, args = {}, {}
    for name in _INS:
        a = _np.ascontiguousarray(inputs[name])
        arrays[f"in_{name}"] = a
        args[name] = nc.dram_tensor(f"in_{name}", a.shape, _mybir.dt.from_np(a.dtype), kind="ExternalInput").ap()
    out = nc.dram_tensor("out_0", (N, D), _mybir.dt.float32, kind="ExternalOutput").ap()
    program(nc, args, out)
    r = _run(nc, [arrays], core_ids=[0])
    return r.results[0]["out_0"]
```

```python
import concourse.bass as bass
from concourse import mybir
from contextlib import ExitStack

N, D, P = 3327, 512, 128
NT = 26
NEG = -9000000000000000.0
HEADS = [1, 8, 4, 1]
FP32 = mybir.dt.float32
I32 = mybir.dt.int32
F32R = mybir.dt.float32r
ALU = mybir.AluOpType
ACT = mybir.ActivationFunctionType
AX = mybir.AxisListType


class Turns:

    def __init__(self, nc, ctx, name):
        self.sems = {(e, n): ctx.enter_context(nc.semaphore(f"{name}_{e}{n}")) for e in ENGINES for n in (1, 16)}
        self.items = []
        self.last = None

    def turn(self, engine, fn, amount=1):
        item = {"engine": engine, "fn": fn, "amount": amount, "wait": None, "to": None}
        if self.last is not None:
            n = self.last["amount"]
            self.last["to"] = item["wait"] = self.sems[engine, n]
        self.items.append(item)
        self.last = item

    def dma(self, fn):
        self.turn("sync", fn, 16)

    def loop(self, count, body):
        self.turn("sync", None)
        outer, self.items = self.items, []
        start = {"engine": "sync", "fn": None, "amount": 1, "wait": None, "to": None}
        self.items.append(start)
        self.last = start
        body()
        self.turn("sync", None)
        inner, self.items = self.items, outer
        self.items.append({"engine": "loop", "count": count, "items": inner})
        after = {"engine": "sync", "fn": None, "amount": 1, "wait": None, "to": None}
        self.items.append(after)
        self.last = after

    def emit(self, e, name, items=None, i=None):
        for item in self.items if items is None else items:
            if item["engine"] == "loop":
                if any(x["engine"] == name for x in item["items"]):
                    with e.Fori(0, item["count"]) as k:
                        self.emit(e, name, item["items"], k)
                continue
            if item["engine"] != name:
                continue
            if item["wait"] is not None:
                e.wait_ge(item["wait"], 16 if item["wait"] is self.sems[name, 16] else 1)
                e.sem_clear(item["wait"])
            last = item["fn"](e, i) if item["fn"] else None
            if item["to"] is not None:
                if last is None:
                    e.sem_inc(item["to"], 1)
                else:
                    last.then_inc(item["to"], item["amount"])


ENGINES = ["sync", "tensor", "vector", "scalar", "gpsimd"]


def rsqrt_steps(y, var, hv, t, wide=False):
    guess = float(0x5F3759DF - (1 << 30) - (1 << 22))
    yield lambda e: e.tensor_scalar(hv, var, 1e-5, -0.5, ALU.add, ALU.mult)
    yield lambda e: e.tensor_scalar(y.bitcast(I32), hv.bitcast(I32), -0.5, guess, ALU.mult, ALU.add)
    for _ in range(3):
        if wide:
            yield lambda e: e.tensor_tensor(t, y, y, ALU.mult)
            yield lambda e: e.tensor_tensor(t, t, hv, ALU.mult)
            yield lambda e: e.scalar_tensor_tensor(y, t, 1.5, y, ALU.add, ALU.mult)
        else:
            yield lambda e: e.tensor_scalar(t, hv, y, y, ALU.mult, ALU.mult)
            yield lambda e: e.tensor_scalar(y, t, 1.5, y, ALU.add, ALU.mult)


def chain_dense(T, nc, g, dr):
    f = g["f"]
    ident, ps, ps2, ps3 = g["ident"], g["ps"], g["ps2"], g["ps3"]
    WE = g["WE"]
    hT = f(0, 4 * N).rearrange("p (k n) -> p k n", n=N)
    WH = f(13312, 26 * D).rearrange("p (t o) -> p t o", o=D)
    base = 13312 * 2
    DB, U = f(base, N), f(base + 3328, N)
    ADJ = f(base + 6656, N).bitcast(I32)
    V = f(base + 9984, N)
    PT = f(base + 13312, NT * P).rearrange("p (t i) -> p t i", i=P)
    base += 13312 + NT * P
    assert base <= g["arena_words"], base
    x0 = base - NT * P
    b2 = 13312 * 2
    XT, YT, VT, H, HT, BI = (f(b2 + D * k, D) for k in range(6))
    W = f(b2 + 3328, 4 * D).rearrange("p (k o) -> p k o", k=4)
    W2 = f(b2 + 3328 + 4 * D, 4 * D).rearrange("p (k o) -> p k o", k=4)
    st = g["small"]
    WDB = f(x0, 4 * P).rearrange("p (k i) -> p k i", i=P)

    def at(e, i):
        return bass.ds(nc.s_assert_within(i * P - ((i + 7) >> 5), 0, N - P, skip_runtime_bounds_check_because="i < 26"), P)

    def add_layer(l, to):
        T.dma(lambda e, i: e.dma_start(XT, (dr["x"] if l <= 1 else dr["XS"][l - 2])[at(e, i), :]))
        if l == 0:
            return
        T.dma(lambda e, i: e.dma_start(YT, dr["Y"][at(e, i), :]))
        if l == 1:
            T.dma(lambda e, i: e.dma_start(VT, dr["V"][at(e, i), :]))
            T.turn("vector", lambda e, i: e.tensor_tensor(YT, YT, VT, ALU.add))
            T.turn("vector", lambda e, i: e.tensor_scalar(YT, YT, 0.0, None, ALU.max))
        if l == 3:
            T.turn("vector", lambda e, i: e.tensor_scalar(VT, YT, 0.0, None, ALU.min))
            T.turn("scalar", lambda e, i: e.activation(VT, VT, ACT.Exp))
            T.turn("vector", lambda e, i: e.tensor_scalar(YT, YT, 0.0, -1.0, ALU.max, ALU.add))
            T.turn("vector", lambda e, i: e.tensor_tensor(YT, YT, VT, ALU.add))
        T.turn("vector", lambda e, i: e.tensor_tensor(XT, XT, YT, ALU.add))
        T.dma(lambda e, i: e.dma_start(to[at(e, i), :], XT))

    for l in range(4):
        NH, F = HEADS[l], D // HEADS[l]
        T.dma(lambda e, i, l=l: e.dma_start(W.rearrange("p k o -> p (k o)"), dr["PW"][0 if l == 0 else l + 1]))
        if l == 0:
            T.dma(lambda e, i: e.dma_start(W2.rearrange("p k o -> p (k o)"), dr["PW"][1]))
            T.dma(lambda e, i: e.dma_start(g["brow"][0:1, 0, :], dr["PB"]))
            T.turn("tensor", lambda e, i: e.matmul(ps, g["ones"][0:1, :], g["brow"][0:1, 0, :], start=True, stop=True))
            T.turn("vector", lambda e, i: e.tensor_copy(BI, ps))

        def nodes(l=l, NH=NH):
            add_layer(l, dr["XS"][l - 1] if l else None)
            T.turn("vector", lambda e, i: e.bn_stats(st[:, 0:6], XT))
            T.turn("vector", lambda e, i: e.bn_aggr(st[:, 6:8], st[:, 0:6]))
            for fn in rsqrt_steps(st[:, 8:9], st[:, 7:8], st[:, 13:14], st[:, 14:15]):
                T.turn("vector", lambda e, i, fn=fn: fn(e))
            T.turn("vector", lambda e, i: e.scalar_tensor_tensor(st[:, 9:10], st[:, 6:7], -1.0, st[:, 8:9], ALU.mult, ALU.mult))
            T.turn("scalar", lambda e, i: e.activation(H, XT, ACT.Relu, bias=st[:, 9:10], scale=st[:, 8:9]))

            def tr(e, i):
                for k in range(4):
                    last = e.transpose(ps[:, k * P:(k + 1) * P], H[:, k * P:(k + 1) * P], ident)
                return last
            T.turn("tensor", tr)
            T.turn("vector", lambda e, i: e.tensor_copy(HT, ps))
            for k in range(4):
                T.dma(lambda e, i, k=k: e.dma_start(dr["HT"][k, :, at(e, i)], HT[:, k * P:(k + 1) * P]))

            def product(w, n, to):
                def mm(e, i):
                    for k in range(4):
                        last = e.matmul(ps[:, 0:n], HT[:, k * P:(k + 1) * P], w(k), start=k == 0, stop=k == 3)
                    return last
                T.turn("tensor", mm)
            product(lambda k: W[:, k, :], D, None)
            T.turn("vector", lambda e, i: e.tensor_copy(YT, ps))
            T.dma(lambda e, i: e.dma_start(dr["WH"][at(e, i), :], YT))
            if l == 0:
                product(lambda k: W2[:, k, :], D, None)
                T.turn("vector", lambda e, i: e.tensor_tensor(YT, ps, BI, ALU.add))
                T.dma(lambda e, i: e.dma_start(dr["V"][at(e, i), :], YT))
            else:
                product(lambda k: WE[:, l - 1, k, 8:8 + NH], NH, None)
                T.turn("vector", lambda e, i: e.tensor_copy(st[:, 16:16 + NH], ps[:, 0:NH]))
                T.dma(lambda e, i: e.dma_start(dr["S"][at(e, i), 0:NH], st[:, 16:16 + NH], allow_slow_non_contiguous=True))

        T.loop(NT, nodes)
        for k in range(4):
            T.dma(lambda e, i, k=k: e.dma_start(hT[:, k, :], dr["HT"][k, :, 0:N]))
        T.dma(lambda e, i: e.dma_start(WH[:, 0:NT - 1, :], dr["WH"][0:(NT - 1) * P, :].rearrange("(t p) o -> p t o", p=P)))
        T.dma(lambda e, i: e.dma_start(WH[0:N - (NT - 1) * P, NT - 1, :], dr["WH"][(NT - 1) * P:N, :]))

        for h in range(NH):
            if l:
                T.turn("vector", lambda e, i, l=l, h=h: e.tensor_copy(
                    WDB, WE[:, l - 1, :, h:h + 1].broadcast_to([P, 4, P])))
                for j in range(0, N, D):
                    n = min(D, N - j)

                    def db(e, i, j=j, n=n):
                        for k in range(4):
                            last = e.matmul(ps[:, 0:n], WDB[:, k, :], hT[:, k, j:j + n], start=k == 0, stop=k == 3)
                        return last
                    T.turn("tensor", db)
                    T.turn("vector", lambda e, i, j=j, n=n: e.tensor_copy(DB[:, j:j + n], ps[:, 0:n]))

            def rows(l=l, h=h, F=F):
                T.dma(lambda e, i: e.dma_start(ADJ, dr["adj"][at(e, i), :]))
                if l == 0:
                    T.turn("vector", lambda e, i: e.tensor_scalar(U, ADJ, 0.0, None, ALU.is_gt))
                    T.turn("vector", lambda e, i: e.tensor_reduce(st[:, 10:11], U, AX.X, ALU.add))
                    T.turn("vector", lambda e, i: e.tensor_scalar(st[:, 10:11], st[:, 10:11], 1.0, None, ALU.max))
                else:
                    T.dma(lambda e, i: e.dma_start(st[:, 15:16], dr["S"][at(e, i), h:h + 1], allow_slow_non_contiguous=True))
                    T.turn("vector", lambda e, i: e.tensor_scalar(U, DB, st[:, 15:16], None, ALU.add))
                    T.turn("vector", lambda e, i: e.scalar_tensor_tensor(U, U, 0.2, U, ALU.mult, ALU.max))
                    if l < 3:
                        T.turn("vector", lambda e, i: e.scalar_tensor_tensor(U, ADJ, 0.0, U, ALU.is_gt, ALU.mult))
                        T.turn("vector", lambda e, i: e.tensor_scalar(V, ADJ, 0.0, NEG, ALU.is_le, ALU.mult))
                    else:
                        T.turn("vector", lambda e, i: e.scalar_tensor_tensor(U, ADJ, 0.0, U, ALU.not_equal, ALU.mult))
                        T.turn("vector", lambda e, i: e.tensor_scalar(V, ADJ, 0.0, NEG, ALU.is_equal, ALU.mult))
                    T.turn("vector", lambda e, i: e.tensor_tensor(U, U, V, ALU.add))
                    T.turn("vector", lambda e, i: e.tensor_reduce(st[:, 11:12], U, AX.X, ALU.max))
                    T.turn("vector", lambda e, i: e.tensor_scalar(st[:, 11:12], st[:, 11:12], -1.0, None, ALU.mult))
                    T.turn("scalar", lambda e, i: e.activation(U, U, ACT.Exp, bias=st[:, 11:12], accum_out=st[:, 10:11]))
                T.turn("vector", lambda e, i: e.reciprocal(st[:, 12:13], st[:, 10:11]))
                for c in range(0, NT, 4):
                    js = [(j, min(P, N - j * P)) for j in range(c, min(c + 4, NT))]

                    def tr(e, i, js=js, c=c):
                        for j, n in js:
                            last = e.transpose(ps[0:n, (j - c) * P:(j - c + 1) * P], U[:, j * P:j * P + n], ident)
                        return last
                    T.turn("tensor", tr)
                    full = [j for j, n in js if n == P]
                    T.turn("vector", lambda e, i, c=c, m=len(full): e.tensor_copy(
                        PT[:, c:c + m, :], ps[:, 0:m * P].rearrange("p (t i) -> p t i", i=P)))
                    for j, n in js[len(full):]:
                        T.turn("vector", lambda e, i, j=j, n=n, c=c: e.tensor_copy(
                            PT[0:n, j, :], ps[0:n, (j - c) * P:(j - c + 1) * P]))

                def mm(e, i):
                    for j in range(NT):
                        n = min(P, N - j * P)
                        last = e.matmul(ps2[:, 0:F], PT[0:n, j, :], WH[0:n, j, h * F:(h + 1) * F],
                                        start=j == 0, stop=j == NT - 1)
                    return last
                T.turn("tensor", mm)
                T.turn("vector", lambda e, i: e.tensor_scalar(V[:, 0:F], ps2[:, 0:F], st[:, 12:13], None, ALU.mult))
                T.dma(lambda e, i: e.dma_start(dr["Y"][at(e, i), h * F:(h + 1) * F], V[:, 0:F]))

            T.loop(NT, rows)
    T.loop(NT, lambda: add_layer(4, dr["out"]))


BF16 = mybir.dt.bfloat16
FP16 = mybir.dt.float16
U8 = mybir.dt.uint8
U32 = mybir.dt.uint32
NC = 5
NK = 16
SEG = 416
NSEG = 8
HALF = 256
ROW = 2 * HALF + 8
WIDE = 2 * HALF + 16
MID = 1664.0
FAR = 4096.0


class Queues:

    def __init__(self, nc, ctx):
        self.nc, self.ctx = nc, ctx
        self.sem = {e: ctx.enter_context(nc.semaphore(f"q_{e}")) for e in ENGINES[1:]}
        self.count = dict.fromkeys(self.sem, 0)
        self.slots = {}
        self.marks = {}
        self.items = {e: [] for e in ENGINES}

    def op(self, engine, fn, key=None):
        if key is not None:
            self.count[engine] += 1
            assert key not in self.marks, key
            self.marks[key] = (self.sem[engine], self.count[engine])
        self.items[engine].append((fn, self.sem[engine] if key is not None else None, 1))

    def dma(self, engine, fn, slot, key):
        if slot not in self.slots:
            self.slots[slot] = [self.ctx.enter_context(self.nc.semaphore(f"d_{slot}")), 0]
        s = self.slots[slot]
        s[1] += 16
        self.marks[key] = (s[0], s[1])
        self.items[engine].append((fn, s[0], 16))

    def wait(self, engine, *keys):
        for key in keys:
            self.items[engine].append((None, key, 0))

    def emit(self, e, name):
        met = {}
        for fn, x, n in self.items[name]:
            if fn is None:
                sem, value = self.marks[x]
                if met.get(id(sem), 0) < value:
                    met[id(sem)] = value
                    e.wait_ge(sem, value)
            else:
                last = fn(e)
                if x is not None:
                    last.then_inc(x, n)


class Thread:

    def __init__(self, a=0.0, b=1.0):
        self.a, self.b = a, b
        self.ops = []

    def __call__(self, fn, *after, key=None, dep=True):
        self.ops.append((fn, after, key, dep))


def merged(Q, *threads):
    threads = [t for t in threads if t.ops]
    at = sorted((t.a + (t.b - t.a) * (n + 0.5) / len(t.ops), k, n) for k, t in enumerate(threads) for n in range(len(t.ops)))
    if Q.count["vector"]:
        Q.wait("vector", merged.last)
    last = {}
    for _, k, n in at:
        fn, after, key, dep = threads[k].ops[n]
        if dep and n:
            Q.wait("vector", last[k])
        Q.wait("vector", *after)
        last[k] = ("v", Q.count["vector"])
        Q.op("vector", fn, last[k])
        if key is not None:
            Q.marks[key] = Q.marks[last[k]]
        merged.last = last[k]


def sparse(Q, nc, g, dr):
    f, psum = g["f"], g["psum"]
    ident, WE = g["ident"], g["WE"]
    V, S, T, G, SP = "vector", "scalar", "tensor", "gpsimd", "sync"
    HALFROW = NSEG * SEG // 2
    NG = 4

    at = [0]

    def take(n, shape=None, dt=None):
        v = f(at[0], n)
        at[0] += n
        if dt is not None:
            v = v.bitcast(dt)
        return v if shape is None else v.rearrange(shape[0], **shape[1])

    X = take(NT * D, ("p (t o) -> p t o", dict(o=D)))
    SbW, STbW = take(NT * 160), take(NT * 160)
    Sb, STb = (v.bitcast(U8).rearrange("p (t e) -> p t e", t=NT) for v in (SbW, STbW))
    K1 = take(NT * 20, ("p (t c k) -> p t c k", dict(c=NC, k=NK)), U8)
    WLF = [take(4 * WIDE) for _ in range(2)]
    W0 = [w[:, 0:4 * D].rearrange("p (k o) -> p k o", k=4) for w in WLF]
    WL = [w.rearrange("p (k a o) -> p k a o", k=4, a=2) for w in WLF]
    IDX = take(NT * 6, ("p (t c) -> p t c", dict(c=6)), U32)
    sm_at = at[0]
    SM = take(2 * NT * 16, ("p (a t h) -> p a t h", dict(a=2, h=16)))
    R = take(NT * NK, ("p (t c) -> p t c", dict(c=NK)))
    DEG, END, FL, RDEG, HS = take(NT), take(NT), take(NT), take(NT), take(4 * NT, ("p (k t) -> p k t", dict(k=4)))
    B3, ones16 = take(HALF, None, BF16), take(P // 2, None, BF16)
    UPPER = take(P)
    K16, EC, ROWID = take(NK), take(NC), take(1)
    hsum, mrow = take(4), take(ROW)
    small = [take(20) for _ in range(2)]
    fl = take(4)
    H = take(D)
    HT = [take(D, ("p (k i) -> p k i", dict(k=4))) for _ in range(2)]
    WO = [take(WIDE) for _ in range(2)]
    shared = at[0]
    ADJ = [take(N + 1) for _ in range(2)]
    S1, S2 = (take(4 * D, ("p (k o) -> p k o", dict(k=4))) for _ in range(2))
    PA, PB = (v[:, NT * 160 - 4 * D:].rearrange("p (k o) -> p k o", k=4) for v in (SbW, STbW))
    FREE = (NT * 160 - 4 * D) // 160
    AB = WO[1][:, 0:D]
    IO = take(HALFROW // 2, None, FP16)
    MARK = [take(HALFROW, None, FP16) for _ in range(2)]
    VO = mrow[:, 0:D]
    E640, A640, STF = (take(320, None, FP16) for _ in range(3))
    assert at[0] <= g["arena_words"], at[0]
    at[0] = sm_at
    TOLD = 18 + P
    R16 = [take(TOLD // 2, None, FP16) for _ in range(2)]
    E18 = take(NC * 18, ("p (c k) -> p c k", dict(c=NC)))
    CAND, CAND2 = take(64), take(64)
    tmp16 = take(NK)
    kk, colf, z5 = take(NC), take(NC), take(NC)
    tmp80 = take(NC * NK, ("p (c k) -> p c k", dict(c=NC)))
    first, final = take(1), take(1)
    ST6, MV = take(NT * 6, ("p (t c) -> p t c", dict(c=6))), take(NT * 2, ("p (t c) -> p t c", dict(c=2)))
    RS, NM, HV, TT = take(NT), take(NT), take(NT), take(NT)
    assert at[0] <= sm_at + 2 * NT * 16
    at[0] = shared
    NEGM = take(NT * NK, ("p (t k) -> p t k", dict(k=NK)))
    GB = [take(NC * WIDE, ("p (c o) -> p c o", dict(c=NC))) for _ in range(NG)]
    ST16 = take(320, None, BF16)
    SM3, rest, Q5 = take(24, None, BF16), take(16), take(80, ("p (c h) -> p c h", dict(c=NC)))
    SELR = [g["sel"][:, k, :] for k in range(3)]
    SEL4 = take(640)
    SEL = [v.bitcast(FP32) for v in SELR] + [SEL4]
    GH, GL = ([g["parts"][:, a, k, :] for k in range(2)] for a in range(2))
    DK = take(NC * NK * 8)
    EM = take(NK * 8)
    U5 = take(NC * 8, ("p (c h) -> p c h", dict(c=NC)))
    Y = take(D)
    VT = [take(D) for _ in range(2)]
    Y2 = VT[0]
    rden, u8 = take(8), take(8)
    assert at[0] <= g["arena_words"], at[0]

    p_q, p_ell, p_t, p_small = psum[:, 0, 0:240], psum[:, 0, 256:384], psum[:, 1, :], psum[:, 4, :]
    p_prep, p_bias = [psum[:, 5, :], psum[:, 6, :]], psum[:, 3, :]
    p_list = [psum[:, 0, 0:3 * TOLD], psum[:, 7, 0:2 * TOLD]]
    p_own = [psum[:, 2, :], psum[:, 3, :]]
    p_num = [psum[:, 2:4, :], psum[:, 4:6, :]]
    p_wh = psum[:, 6:8, 0:HALF + 8]

    def rows(t):
        return min(P, N - t * P)

    def parts(t):
        return [(0, P)] if t < NT - 1 else [(0, 112), (112, rows(t))]

    def pool(fn, key, *after):
        if pool.last:
            Q.wait(G, pool.last)
        Q.wait(G, *after)
        Q.op(G, fn, key)
        pool.last = key
    pool.last = None

    def iota(out, pattern, base, mult, key):
        pool(lambda e: e.iota(out, pattern=pattern, base=base, channel_multiplier=mult,
                              allow_small_or_imprecise_dtypes=True), key)

    def pieces(engine, dst, src, t, slot, key):
        keys = []
        for q, (a, b) in enumerate(parts(t)):
            Q.dma(engine, lambda e, a=a, b=b: e.dma_start(dst(a, b), src(a, b)), f"{slot}_{q}", (*key, q))
            keys.append((*key, q))
        return keys

    def done(key, t):
        return [(*key, q) for q in range(len(parts(t)))]

    def load_adj(t):
        if t >= 2:
            Q.wait(SP, ("mark", t - 2))
        if t == NT - 1:
            Q.wait(SP, "adjpad")
        buf = ADJ[t % 2].bitcast(I32)
        pieces(SP, lambda a, b: buf[a:b, 0:N], lambda a, b: dr["adj"][t * P + a:t * P + b, :], t, f"adj{t % 2}", ("adj", t))

    def weights(l, key):
        slot, which = (l + 1) % 2, l + 1
        Q.wait(SP, ("pwout", which), *([("pwout", 0), ("pwout", 1)] if l < 3 else []))
        src = dr["PW"][which].rearrange("p (k a o) -> p k a o", k=4, a=2)
        for a in range(2):
            Q.dma(SP, lambda e, a=a: e.dma_start(WL[slot][:, :, a, 0:HALF], src[:, :, a, :]), f"wl{slot}{a}", (*key, a))

    def natural(x):
        return x.rearrange("(k p) o -> p k o", p=P)

    def prep_load(fn, slot, key, *after, engine=G):
        Q.wait(engine, *after)
        Q.dma(engine, fn, slot, key)

    def prep_loads(which):
        w, b = (("W_nb", "b_nb"), ("W_self", "b_self"))[which]
        half = D * (1 - which)
        engine = G if which else SP
        prep_load(lambda e: e.dma_start(PA, natural(dr[w])), f"pa{which}", ("pal", which), *([("ptr", 0, 3)] if which else []), engine=engine)
        prep_load(lambda e: e.dma_start((PB, S2)[which], natural(dr["W_comb"][half:half + D, :])), f"pb{which}", ("pbl", which),
                  engine=engine)
        prep_load(lambda e: e.dma_start(g["bcol"], dr[b].rearrange("(k p) -> p k", p=P), allow_slow_non_contiguous=True),
                  f"pbc{which}", ("pbc", which), *([("pbias", 0)] if which else []), engine=engine)

    WEall = WE.rearrange("p l k h -> p (l k h)")
    pool(lambda e: e.memset(ident, 0.0), "ident0")
    pool(lambda e: e.affine_select(out=ident, in_=ident, compare_op=ALU.not_equal, fill=1.0, base=0,
                                   pattern=[[-1, P]], channel_multiplier=1), "ident")
    pool(lambda e: e.memset(X[96:P, NT - 1, :], 0.0), "xpad")
    for m in range(2):
        pool(lambda e, m=m: e.memset(MARK[m], 0.0), ("mark0", m))
    iota(IO, [[1, HALFROW]], 1, 0, "io")
    iota(E640, [[1, NC * P]], 0, 0, "e640")
    iota(K16, [[1, NK]], 0, 0, "k16")
    iota(EC, [[P, NC]], 0, 1, "ec")
    iota(ROWID, [[0, 1]], 1, 1, "rowid")
    pool(lambda e: e.memset(UPPER, 1.0), "upper0")
    pool(lambda e: e.affine_select(out=UPPER, in_=UPPER, compare_op=ALU.is_gt, fill=0.0, base=0,
                                   pattern=[[1, P]], channel_multiplier=-1), "upper")
    pool(lambda e: e.memset(mrow, 0.0), "mrow0")
    for r16 in R16:
        pool(lambda e, r16=r16: e.memset(r16[:, 18:], 0.0), ("told0", id(r16)))
        pool(lambda e, r16=r16: e.affine_select(out=r16[:, 18:], in_=r16[:, 18:], compare_op=ALU.not_equal, fill=1.0, base=0,
                                                pattern=[[-1, P]], channel_multiplier=1), "told" if r16 is R16[1] else ("told1",))

    pool(lambda e: e.memset(g["ones"], 1.0), "ones")
    pool(lambda e: e.memset(WEall, 0.0), "we0")
    pool(lambda e: e.memset(ones16, 1.0), "ones16")

    Q.dma(SP, lambda e: e.dma_start(g["brow"][0:1, 1, :], dr["b_comb"].rearrange("(a n) -> a n", a=1)), "bcomb", "bcomb")
    load_adj(0)
    prep_loads(0)
    load_adj(1)
    GROUPS = [(0, 5), (5, 13), (13, NT)]

    def load_x(k):
        a, b = GROUPS[k]
        b = min(b, NT - 1)
        Q.dma(SP, lambda e: e.dma_start(X[:, a:b, :], dr["x"][a * P:b * P, :].rearrange("(t p) o -> p t o", p=P)), f"x{k}", ("x", k))
        if k == 2:
            Q.wait(SP, "xpad")
            pieces(SP, lambda a, b: X[a:b, NT - 1, :], lambda a, b: dr["x"][(NT - 1) * P + a:(NT - 1) * P + b, :], NT - 1, "xc", ("xc",))

    load_x(0)
    Q.wait(SP, "mrow0")
    Q.dma(SP, lambda e: e.dma_start(dr["T"][0][N:N + 1, :], mrow[0:1, 0:D]), "zero", "zero")

    def first_norm(t0, t1, key, *after):
        v = Thread()
        for t in range(t0, t1):
            v(lambda e, t=t: e.bn_stats(ST6[:, t, :], X[:, t, :]), *(after if t == t0 else []), dep=False)
        for t in range(t0, t1):
            v(lambda e, t=t: e.bn_aggr(MV[:, t, :], ST6[:, t, :]), dep=t == t0)
        for fn in rsqrt_steps(RS[:, t0:t1], MV[:, t0:t1, 1], HV[:, t0:t1], TT[:, t0:t1], True):
            v(fn)
        v(lambda e: e.scalar_tensor_tensor(NM[:, t0:t1], MV[:, t0:t1, 0], -1.0, RS[:, t0:t1], ALU.mult, ALU.mult), key=key)
        return v

    def prep_bank(key, fn, after, out):
        bank = p_prep[len(prep_bank.keys) % 2]
        if len(prep_bank.keys) >= 2:
            Q.wait(T, prep_bank.keys[-2])
        Q.wait(T, *after)
        for c in range(4):
            Q.op(T, lambda e, c=c: fn(e, bank, c), key if c == 3 else None)
        Q.wait(S, key, *out[2])
        Q.op(S, lambda e: e.activation(out[1], bank, ACT.Copy), out[0])
        prep_bank.keys.append(out[0])
    prep_bank.keys = []

    def prep_transposed(name, src, dst, loaded, free):
        for k in range(4):
            prep_bank(("ptr", name, k),
                      lambda e, bank, c, k=k: e.transpose(bank[:, c * P:(c + 1) * P], src[:, c, k * P:(k + 1) * P], ident),
                      [loaded, "ident"], (("pc", name, k), dst[:, k, :], free))

    def prep_product(which, k):
        prep_bank(("pm", which, k),
                  lambda e, bank, c: e.matmul(bank, S1[:, c, k * P:(k + 1) * P], (PB, S2)[which][:, c, :], start=c == 0, stop=c == 3),
                  [("pc", which, 3), ("pbl", which)], (("pw", which, k), W0[which][:, k, :], []))
        if k == 3:
            Q.marks["w", 10 * which] = Q.marks["pw", which, 3]

    def prep_bias(which):
        Q.wait(T, ("pbc", which), ("pbl", which))
        for c in range(4):
            Q.op(T, lambda e, c=c: e.matmul(p_bias[0:1, :], g["bcol"][:, c:c + 1], (PB, S2)[which][:, c, :], start=which == 0 and c == 0,
                                            stop=False), ("pbias", which) if c == 3 else None)
        if which:
            Q.wait(T, "bcomb", "ones")
            Q.op(T, lambda e: e.matmul(p_bias[0:1, :], g["ones"][0:1, 0:1], g["brow"][0:1, 1, :], start=False, stop=True), "pbsum")
            Q.wait(S, "pbsum")
            Q.op(S, lambda e: e.activation(g["brow"][0:1, 0, :], p_bias[0:1, :], ACT.Copy), "bias0")

    def prep_out(which):
        src = W0[which] if which < 2 else S1
        prep_load(lambda e: e.dma_start(dr["PW"][which], src.rearrange("p k o -> p (k o)")), f"pw{which}", ("pwout", which),
                  *([("pw", which, 3)] if which < 2 else []))

    def prep_scores(l, s, *ready):
        NH, F = HEADS[l], D // HEADS[l]
        if l < 3:
            src = dr[f"a{l}"][:, s * F:(s + 1) * F].rearrange("(q h) o -> q h o", q=1)
        else:
            src = dr[f"a3{s}"].rearrange("(q h o) -> q h o", q=1, h=1)
        prep_load(lambda e: e.dma_start(AB.rearrange("p (h o) -> p h o", h=NH), src.broadcast_to([P, NH, F])), "ab", ("ab", l, s), *[("bias", k) for k in range(3)])
        pool(lambda e: e.tensor_tensor(S2, S1, AB.unsqueeze(1).broadcast_to([P, 4, D]), ALU.mult), ("pmul", l, s),
             ("ab", l, s), *ready)

    def prep_reduce(l, s):
        v = Thread()
        NH, F = HEADS[l], D // HEADS[l]
        v(lambda e: e.tensor_reduce(WE[:, l - 1, :, 8 - 8 * s:8 - 8 * s + NH], S2.rearrange("p k (h o) -> p k h o", o=F), AX.X, ALU.add),
          ("pmul", l, s), "we0", key=("pred", l, s))
        return v

    def prep_bias_parts():
        whole, rest = g["brow"][0:1, 0, :], g["brow"][0:1, 1, :]
        part = [AB[0:1, 0:HALF].bitcast(BF16), AB[0:1, HALF:D].bitcast(BF16), VO[0:1, 0:HALF].bitcast(BF16)]
        pool(lambda e: e.tensor_copy(part[0], whole), "part0", "bias0")
        pool(lambda e: e.tensor_tensor(rest, whole, part[0], ALU.subtract), "rest0")
        pool(lambda e: e.tensor_copy(part[1], rest), "part1")
        pool(lambda e: e.tensor_tensor(part[2], rest, part[1], ALU.subtract), "part2", "zero")
        for k in range(3):
            prep_load(lambda e, k=k: e.dma_start(B3[k:k + 1, :], part[k]), f"b3{k}", ("bias", k), "part2")

    def prep_later():
        prep_out(0)
        prep_out(1)
        Q.dma(G, lambda e: e.dma_start(dr["PB"], g["brow"][0:1, 0, :]), "pbout", "pbout")
        for h in range(8):
            prep_load(lambda e, h=h: e.dma_start(S1[:, :, h * 64:(h + 1) * 64], natural(dr["W1"][h])), f"s1_{h}", ("s1", h),
                      ("pm", 1, 3))
        prep_scores(1, 0, *[("s1", h) for h in range(8)], ("pm", 1, 3), ("pbias", 1))
        prep_out(2)
        Q.wait(G, ("pmul", 1, 0))
        prep_scores(1, 1, ("pred", 1, 0))
        raw = S2[:, 0, :].rearrange("p (h o) -> p h o", h=4)
        prep_load(lambda e: e.dma_start(raw, dr["W2"].rearrange("h p o -> p h o")), "w2", "w2", ("pred", 1, 1))
        parts4 = [[(0, 1), (1, -1), (2, -1), (3, -1)], [(1, 1), (0, 1), (3, -1), (2, 1)],
                  [(2, 1), (3, 1), (0, 1), (1, -1)], [(3, 1), (2, -1), (1, 1), (0, 1)]]
        for q in range(4):
            for b in range(4):
                c, sign = parts4[q][b]
                dst = S1[:, b, :].rearrange("p (h q o) -> p h q o", h=4, q=4)[:, :, q, :]
                pool(lambda e, dst=dst, c=c, sign=sign: e.tensor_scalar(dst, raw[:, :, c * 32:(c + 1) * 32], float(sign), None, ALU.mult),
                     ("ham", q, b), "w2", ("pwout", 2))
        Q.wait(G, ("ham", 3, 3))
        prep_out(3)
        prep_scores(2, 0)
        Q.wait(G, ("pmul", 2, 0))
        prep_scores(2, 1, ("pred", 2, 0))
        prep_load(lambda e: e.dma_start(S2, natural(dr["W3"])), "w3", "w3", ("pred", 2, 1))
        prep_scores(3, 0, ("pc", 3, 3))
        prep_out(4)
        Q.wait(G, ("pmul", 3, 0))
        prep_scores(3, 1, ("pred", 3, 0))

    def node_h(t, m, scale, bias, *after):
        n = rows(t)
        Q.wait(S, *after)
        if m:
            Q.wait(S, ("tr", m - 1))
        Q.op(S, lambda e: e.activation(H[0:n, :], X[0:n, t, :], ACT.Relu, bias=bias[0:n, :], scale=scale[0:n, :]), ("h", m))

    def node_tr(t, m):
        n = rows(t)
        Q.wait(T, ("h", m))
        if m:
            Q.wait(T, ("ht", m - 1))
        for k in range(4):
            Q.op(T, lambda e, k=k: e.transpose(p_t[:, k * P:k * P + n], H[0:n, k * P:(k + 1) * P], ident[0:n, 0:n]),
                 ("tr", m) if k == 3 else None)

    def node_ht(t, m, sums):
        n = rows(t)
        ht = HT[m % 2]
        Q.wait(S, ("tr", m))
        if m >= 2:
            Q.wait(S, ("proj", m - 2))
        if sums:
            for k in range(4):
                Q.op(S, lambda e, k=k: e.activation(ht[:, k, 0:n], p_t[:, k * P:k * P + n], ACT.Copy,
                                                    accum_out=HS[:, k, t:t + 1]), ("ht", m) if k == 3 else None)
        else:
            Q.op(S, lambda e: e.activation(ht[:, :, 0:n], p_t.rearrange("p (k i) -> p k i", k=4)[:, :, 0:n], ACT.Copy),
                 ("ht", m))

    def mark(t):
        Q.wait(S, *done(("adj", t), t), ("mark0", t % 2))
        if t >= 2:
            Q.wait(S, ("scan", t - 2))
        Q.op(S, lambda e: e.activation(MARK[t % 2][:, 0:N], ADJ[t % 2].bitcast(I32)[:, 0:N], ACT.Sign), ("mark", t))

    def scan(t):
        v = Thread()
        mk = MARK[t % 2]
        v(lambda e: e.tensor_tensor(mk.rearrange("p (a n) -> p a n", a=2), mk.rearrange("p (a n) -> p a n", a=2),
                                    IO.unsqueeze(1).broadcast_to([P, 2, HALFROW]), ALU.mult), ("mark", t), "io")
        for s in range(NSEG):
            v(lambda e, s=s: e.max(CAND[:, s * 8:s * 8 + 8], mk[:, s * SEG:(s + 1) * SEG]), dep=s == 0,
              key=("scan", t) if s == NSEG - 1 else None)
        r = R[:, t, :]
        v(lambda e: e.tensor_scalar(CAND2[:, 32:64], CAND[:, 32:64], 0.0, float(HALFROW), ALU.is_gt, ALU.mult))
        v(lambda e: e.tensor_reduce(FL[:, t:t + 1], CAND.rearrange("p (s k) -> p s k", k=8)[:, :, 7], AX.X, ALU.max), dep=False)
        v(lambda e: e.tensor_tensor(CAND[:, 32:64], CAND[:, 32:64], CAND2[:, 32:64], ALU.add))
        v(lambda e: e.max(r[:, 0:8], CAND))
        v(lambda e: e.match_replace(CAND2, r[:, 0:8], CAND, 0.0))
        v(lambda e: e.max(r[:, 8:16], CAND2))
        v(lambda e: e.tensor_scalar(tmp16, r[:, 0:16], 0.0, 0.0, ALU.is_gt, ALU.add, accum_out=DEG[:, t:t + 1]))
        v(lambda e: e.tensor_scalar(tmp16[:, 0:1], DEG[:, t:t + 1], 0.0, float(N + 1), ALU.is_equal, ALU.mult))
        v(lambda e: e.tensor_scalar(DEG[:, t:t + 1], DEG[:, t:t + 1], 1.0, None, ALU.max), key=("deg", t))
        v(lambda e: e.tensor_tensor(r[:, 0:1], r[:, 0:1], tmp16[:, 0:1], ALU.add), key=("r", t), dep=False)
        return v

    def off(t):
        Q.wait(T, ("deg", t), "upper")
        if t:
            Q.wait(T, ("end", t - 1))
        Q.op(T, lambda e: e.matmul(p_small[:, 0:1], UPPER, DEG[:, t:t + 1], start=True, stop=True), ("off", t))

    def spread(t):
        v = Thread(0.3, 0.8)
        r = R[:, t, :]
        r16 = R16[t % 2]
        v(lambda e: e.tensor_scalar(r16[:, 0:NK], r[:, 0:NK], -MID, None, ALU.add), ("r", t), *([("edges", t - 2)] if t >= 2 else []))
        v(lambda e: e.tensor_copy(r16[:, 17:18], ROWID), "rowid", dep=False)
        v(lambda e: e.tensor_copy(r16[:, 16:17], p_small[:, 0:1]), ("off", t), dep=False)
        v(lambda e: e.tensor_tensor(END[:, t:t + 1], DEG[:, t:t + 1], p_small[:, 0:1], ALU.add), dep=False)
        v(lambda e: e.tensor_copy(first, p_small[:, 0:1]), dep=False)
        v(lambda e: e.scalar_tensor_tensor(final, DEG[:, t:t + 1], -1.0, p_small[:, 0:1], ALU.add, ALU.add), key=("end", t), dep=False)
        v(lambda e: e.tensor_scalar(A640, E640, first, final, ALU.max, ALU.min), "e640")
        v(lambda e: e.tensor_tensor(STF, A640, E640, ALU.is_equal),
          *([("stb", t - 1), ("edges", t - 1)] if t else []), key=("stf", t))
        return v

    def lists(t):
        v = Thread(0.25, 1.0)
        pe = E18
        v(lambda e: e.tensor_tensor(kk, EC, pe[:, :, 16], ALU.subtract), ("e18", t), "ec")
        v(lambda e: e.tensor_tensor(K1[:, t, :, :], K16.unsqueeze(1).broadcast_to([P, NC, NK]),
                                    kk.unsqueeze(2).broadcast_to([P, NC, NK]), ALU.is_equal))
        v(lambda e: e.tensor_scalar(z5, pe[:, :, 17], 0.0, FAR, ALU.is_equal, ALU.mult), dep=False)
        v(lambda e: e.tensor_tensor(tmp80, K1[:, t, :, :], pe[:, :, 0:NK], ALU.mult))
        v(lambda e: e.tensor_reduce(colf, tmp80, AX.X, ALU.add))
        v(lambda e: e.scalar_tensor_tensor(IDX[:, t, 0:NC], colf, MID - 1.0, z5, ALU.add, ALU.add), key=("idx", t))
        return v

    def edges(t):
        Q.wait(T, ("stf", t), "told")
        if t:
            Q.wait(T, ("sb", t - 1))
        for c in range(NC):
            Q.op(T, lambda e, c=c: e.matmul(p_list[c // 3][:, c % 3 * TOLD:(c % 3 + 1) * TOLD], STF[:, c * P:(c + 1) * P], R16[t % 2], start=True, stop=True),
                 ("edges", t) if c == NC - 1 else None)

    def stb(t):
        Q.wait(S, ("edges", t), *([("idx", t - 1)] if t else []))
        both = [(0, 3, p_list[0]), (3, NC, p_list[1])]
        told = [(a, b, p.rearrange("p (c k) -> p c k", k=TOLD)) for a, b, p in both]
        for a, b, p in told:
            Q.op(S, lambda e, a=a, b=b, p=p: e.activation(E18[:, a:b, :], p[:, :, 0:18], ACT.Copy), ("e18", t) if a else None)
        Q.wait(S, *([("pm", 1, 3), ("pbias", 1)] if t >= FREE else []))
        for a, b, p in told:
            Q.op(S, lambda e, a=a, b=b, p=p: e.activation(Sb[:, t, a * P:b * P].rearrange("p (c i) -> p c i", i=P), p[:, :, 18:],
                                                          ACT.Copy), ("sb", t) if a else None)
        Q.wait(S, ("stf", t))
        Q.op(S, lambda e: e.activation(STb[:, t, :], STF, ACT.Copy), ("stb", t))

    def own(t, which, part):
        n = rows(t)
        key = ("pa", "pb")[which]
        dst = p_own[which]
        if part == 0:
            Q.wait(T, ("ht", t), ("w", 10 * which), *[("bias", k) for k in range(3)], "ones16")
            if t:
                Q.wait(T, (("wo", "vo")[which], t - 1))
        for k in (2 * part, 2 * part + 1):
            last = k == 3 and which == 0
            Q.op(T, lambda e, k=k, last=last: e.matmul(dst[0:n, :], HT[t % 2][:, k, 0:n], W0[which][:, k, :], start=k == 0,
                                                       stop=last), (key, t) if last else None)
        if which and part:
            Q.op(T, lambda e: e.matmul(dst[0:n, :], ones16[0:3, 0:n], B3[0:3, :], start=False, stop=True), (key, t))
            Q.marks["proj", t] = Q.marks[key, t]

    def own_out(t, which):
        n = rows(t)
        buf = VO if which else WO[0]
        dst = p_own[which]
        name = ("tout", "vout")[which]
        Q.wait(S, (("pa", "pb")[which], t))
        Q.wait(S, *(done((name, 0, t - 1), t - 1) if t else ["zero"]))
        Q.op(S, lambda e: e.activation(buf[0:n, 0:D], dst[0:n, :], ACT.Copy), (("wo", "vo")[which], t))
        Q.wait(SP, (("wo", "vo")[which], t))
        to = dr["V"] if which else dr["T"][0]
        pieces(SP, lambda a, b: to[t * P + a:t * P + b, :], lambda a, b: buf[a:b, 0:D], t, name, (name, 0, t))

    def first_h(t):
        node_h(t, t, RS[:, t:t + 1], NM[:, t:t + 1], ("ln0", [a <= t < b for a, b in GROUPS].index(True)))

    def unit(t, which, part):
        if t == 0 and which == part == 0:
            first_h(0)
            node_tr(0, 0)
            node_ht(0, 0, False)
            first_h(1)
        own(t, which, part)
        if part:
            own_out(t, which)
        if (which, part) == (0, 0) and t + 1 < NT:
            node_tr(t + 1, t + 1)
            node_ht(t + 1, t + 1, False)
            if t + 2 < NT:
                first_h(t + 2)

    work = [(1.7, lambda: prep_transposed(0, PA, S1, ("pal", 0), []))]
    work += [(3.5, lambda k=k: prep_product(0, k)) for k in range(4)]
    work += [(3.5, lambda: prep_bias(0)), (1.7, lambda: prep_transposed(1, PA, S1, ("pal", 1), [("pm", 0, 3)]))]
    work += [(3.5, lambda k=k: prep_product(1, k)) for k in range(4)]
    work += [(4.4, lambda: prep_bias(1))]
    work += [(2.2, lambda u=(t, which, part): unit(*u)) for t in range(NT) for which in range(2) for part in range(2)]
    total = sum(w for w, _ in work)
    prep_loads(1)
    prep_bias_parts()
    prep_later()
    reduces = {7: (1, 0), 9: (1, 1), 12: (2, 0), 14: (2, 1), 18: (3, 0), 20: (3, 1)}
    norms = {2: 0, 5: 1, 8: 2}
    mark(0)
    spent = 0.0
    LAG = 2
    for t in range(NT + LAG + 1):
        mine = []
        while work and spent + work[0][0] <= total * (t + 1) / NT + 0.01:
            spent += work[0][0]
            mine.append(work.pop(0)[1])
        if t + 2 < NT:
            load_adj(t + 2)
        if t in (1, 3):
            load_x((t + 1) // 2)
        if t + 1 == NT - 2:
            pool(lambda e: e.memset(ADJ[(NT - 1) % 2][96:P, :], 0.0), "adjpad", ("mark", NT - 3))
        if 0 <= t - LAG < NT:
            off(t - LAG)
        if 0 <= t - LAG - 1 < NT:
            edges(t - LAG - 1)
            stb(t - LAG - 1)
        if t + 1 < NT:
            mark(t + 1)
        for fn in mine[:len(mine) // 2]:
            fn()
        for fn in mine[len(mine) // 2:]:
            fn()
        if t == 16:
            prep_transposed(3, S2, S1, "w3", [("pwout", 3), ("pmul", 2, 1)])
        merged(Q, *([scan(t)] if t < NT else []), *([spread(t - LAG)] if 0 <= t - LAG < NT else []),
               *([lists(t - LAG - 1)] if 0 <= t - LAG - 1 < NT else []),
               *([first_norm(*GROUPS[norms[t]], ("ln0", norms[t]), ("x", norms[t]),
                             *(["xpad", *done(("xc",), NT - 1)] if norms[t] == 2 else []))] if t in norms else []),
               *([prep_reduce(*reduces[t])] if t in reduces else []))

    def clear(places):
        v = Thread()
        for s, c in places:
            v(lambda e, s=s, c=c: e.memset(GB[s][:, c, :], 0.0), ("idx", NT - 1), ("stb", NT - 1), ("mark", NT - 1),
              ("vo", NT - 1), *done(("vout", 0, NT - 1), NT - 1), ("pwout", 4), ("pmul", 3, 1), ("pm", 1, 3), key=("g0", s, c), dep=False)
        return v

    merged(Q, clear([(0, c) for c in range(NC)]))

    end = Thread()
    end(lambda e: e.tensor_reduce(fl[:, 0:1], FL, AX.X, ALU.max), ("idx", NT - 1))
    end(lambda e: e.tensor_reduce(fl[:, 1:2], R[:, :, 15], AX.X, ALU.max), dep=False)
    end(lambda e: e.tensor_reduce(fl[:, 2:3], END, AX.X, ALU.max), dep=False)
    end(lambda e: e.reciprocal(RDEG, DEG), dep=False)
    end(lambda e: e.tensor_scalar(fl[:, 2:3], fl[:, 2:3], float(NC * P), None, ALU.is_gt))
    end(lambda e: e.tensor_reduce(fl[:, 3:4], fl[:, 0:3], AX.X, ALU.max), key="fl")
    Q.wait(T, "fl", ("end", NT - 1))
    Q.op(T, lambda e: e.matmul(p_small[:, 0:1], g["ones"], fl[:, 3:4], start=True, stop=True), "flag0")
    end(lambda e: e.tensor_scalar(g["flag"], p_small[:, 0:1], 0.5, None, ALU.is_gt), "flag0", key="flag")
    merged(Q, end)
    last = clear([(s, c) for s in range(1, NG) for c in range(NC)])
    last(lambda e: e.memset(VT[(NT - 1) % 2][96:P, :], 0.0), key="vpad", dep=False)
    last(lambda e: e.memset(SM.rearrange("p a t h -> p (a t h)"), 0.0), key="sm0", dep=False)
    last(lambda e: e.memset(mrow[0:1, HALF:HALF + 8], 0.0), key="mrowz", dep=False)
    last(lambda e: e.tensor_tensor(NEGM, K16.unsqueeze(1).broadcast_to([P, NT, NK]), DEG.unsqueeze(2).broadcast_to([P, NT, NK]),
                                   ALU.is_ge), "k16", dep=False)
    last(lambda e: e.tensor_scalar(NEGM, NEGM, -1e30, None, ALU.mult))
    merged(Q, last)

    def layer(l):
        NH, F = HEADS[l], D // HEADS[l]
        width = ROW if l else D
        par = l % 2
        if l < 3:
            Q.wait(SP, ("mean", l - 1) if l >= 1 else ("proj", NT - 1), ("proj", NT - 1))
            weights(l + 1, ("w", l + 1))
            Q.wait(S, ("mean", l - 1) if l >= 1 else ("proj", NT - 1), ("proj", NT - 1))
            for a in range(2):
                Q.op(S, lambda e, a=a: e.activation(WL[l % 2][:, :, a, HALF:HALF + 8], WE[:, l, :, 8 * a:8 * a + 8], ACT.Copy),
                     ("we", l + 1) if a else None)

        def gather(t):
            i, s = l * NT + t, t % NG
            if t == 0:
                Q.wait(G, *[k for u in range(NT) for k in done(("tout", l, u), u)], ("meanout", l) if l else "zero",
                       ("idx", NT - 1))
            before = i - NG if t >= NG else (l - 1) * NT + max(u for u in range(NT) if u % NG == s)
            for c in range(NC):
                Q.wait(G, ("used", before, c) if before >= 0 else ("g0", s, c))
                Q.dma(G, lambda e, c=c: e.indirect_dma_start(
                    GB[s][:, c, 0:width], None, dr["T"][l],
                    bass.IndirectOffsetOnAxis(ap=IDX[:, t, c:c + 1], axis=0), bounds_check=N, oob_is_err=False),
                    f"g{s}{c}", ("g", i, c))

        def sel(t):
            i = l * NT + t
            if l == 0:
                to = SELR[i % 3]
                if i >= 3:
                    Q.wait(S, ("num", i - 3))
            else:
                to = (SELR + [SEL4])[i % 4]
                Q.wait(S, ("num", max(i - 4, NT - 1)))
                if i == NT:
                    Q.wait(S, ("g0", 0, 0))
            Q.op(S, lambda e: e.activation(to, Sb[:, t, :], ACT.Copy), ("sel", i))

        def high(t, c):
            j = t * len(APART) + APART.index(c)
            Q.wait(S, ("g", t, c), *([("mm", j - 2)] if j >= 2 else []))
            Q.op(S, lambda e: e.activation(GH[j % 2], GB[t % NG][:, c, 0:D], ACT.Copy), ("high", j))

        def low(t, chunks, a, b):
            v = Thread(a, b)
            for c in chunks:
                j = t * len(APART) + APART.index(c)
                v(lambda e, j=j, c=c: e.tensor_tensor(GL[j % 2], GB[t % NG][:, c, 0:D], GH[j % 2].bitcast(FP32), ALU.subtract),
                  ("high", j), *([("mm", j - 2)] if j >= 2 else []), key=("used", t, c), dep=False)
            return v

        def sums_apart(t, c):
            to, at = p_num[t % 2][:, 0, :], SELR[t % 3][:, c * P:(c + 1) * P]
            first, last = c == 0, c == NC - 1
            if first:
                Q.wait(T, ("sel", t), *([("y", t - 2)] if t >= 2 else ["flag"]))
            if c in APART:
                j = t * len(APART) + APART.index(c)
                Q.wait(T, ("high", j))
                Q.op(T, lambda e: e.matmul(to, at, GH[j % 2], start=first, stop=False))
                Q.wait(T, ("used", t, c))
                Q.op(T, lambda e: e.matmul(to, at, GL[j % 2], start=False, stop=last), ("mm", j))
                done_at = ("mm", j)
            else:
                Q.wait(T, ("g", t, c))
                Q.op(T, lambda e: e.matmul(to, at.bitcast(FP32), GB[t % NG][:, c, 0:D], start=first, stop=last), ("used", t, c))
                done_at = ("used", t, c)
            if last:
                Q.marks["num", t] = Q.marks[done_at]

        def st32(t):
            i = l * NT + t
            if i == NT:
                Q.wait(S, ("g0", 0, 0))
            if i > NT:
                Q.wait(S, ("sme", i - 1))
            Q.op(S, lambda e: e.activation(ST16, STb[:, t, :], ACT.Copy), ("st32", i))

        def scores(t):
            v = Thread(0.9, 0.95) if early else Thread(0.15, 0.2)
            i, s = l * NT + t, t % NG
            d = GB[s][:, :, HALF:HALF + NH]
            dk = DK[:, 0:NC * NK * NH].rearrange("p (c k h) -> p c k h", c=NC, k=NK)
            v(lambda e: e.tensor_tensor(dk, K1[:, t, :, :].unsqueeze(3).broadcast_to([P, NC, NK, NH]),
                                        d.unsqueeze(2).broadcast_to([P, NC, NK, NH]), ALU.mult),
              *[("g", i, c) for c in range(NC)], *([("ell", i - 1)] if i > NT else []), key=("dk", i))
            return v

        def highest(t):
            v = Thread(0.55, 0.95)
            i = l * NT + t
            em = EM[:, 0:NK * NH].rearrange("p (k h) -> p k h", k=NK)
            v(lambda e: e.tensor_tensor(em, p_ell[:, 0:NK * NH].rearrange("p (k h) -> p k h", k=NK),
                                        NEGM[:, t, :].unsqueeze(2).broadcast_to([P, NK, NH]), ALU.add), ("ell", i), key=("em", i))
            v(lambda e: e.tensor_reduce(u8[:, 0:NH], EM[:, 0:NK * NH].rearrange("p (k h) -> p h k", k=NK), AX.X, ALU.max))
            sm = SM[:, par, t, :]
            v(lambda e: e.tensor_tensor(u8[:, 0:NH], u8[:, 0:NH], sm[:, 0:NH], ALU.add), ("sm", l, t), "sm0")
            v(lambda e: e.scalar_tensor_tensor(sm[:, 8:8 + NH], u8[:, 0:NH], 0.2, u8[:, 0:NH], ALU.mult, ALU.max))
            v(lambda e: e.tensor_copy(SM3[:, 0:16], sm), *([("sme", i - 1)] if i > NT else []))
            v(lambda e: e.tensor_tensor(rest, sm, SM3[:, 0:16], ALU.subtract))
            v(lambda e: e.tensor_copy(SM3[:, 16:32], rest))
            v(lambda e: e.tensor_tensor(SM3[:, 32:48], rest, SM3[:, 16:32], ALU.subtract), key=("m8", i))
            return v

        def less_highest(t):
            v = Thread(0.35, 0.6)
            i, s = l * NT + t, t % NG
            d = GB[s][:, :, HALF:HALF + NH]
            v(lambda e: e.tensor_reduce(Q5, p_q.rearrange("p (c a h) -> p c h a", c=NC, a=3), AX.X, ALU.add), ("sme", i),
              *([("ell", i + 1)] if t + 1 < NT else []), key=("q5", i))
            v(lambda e: e.tensor_tensor(U5[:, :, 0:NH], d, Q5[:, :, 0:NH], ALU.add), *([("exp", i - 1)] if i > NT else []))
            v(lambda e: e.scalar_tensor_tensor(U5[:, :, 0:NH], U5[:, :, 0:NH], 0.2, U5[:, :, 0:NH], ALU.mult, ALU.max))
            v(lambda e: e.tensor_tensor(U5[:, :, 0:NH], U5[:, :, 0:NH], Q5[:, :, 8:8 + NH], ALU.subtract))
            v(lambda e: e.tensor_scalar(U5[:, :, 0:NH], U5[:, :, 0:NH], 0.0, None, ALU.min), key=("u5", i))
            return v

        def ell(t, c):
            i = l * NT + t
            if c == 0:
                Q.wait(T, ("dk", i), ("sel", i), *([("em", i - 1)] if i > NT else []))
            Q.op(T, lambda e: e.matmul(p_ell[:, 0:NK * NH], SEL[i % 4][:, c * P:(c + 1) * P],
                                       DK[:, c * NK * NH:(c + 1) * NK * NH],
                                       start=c == 0, stop=c == NC - 1), ("ell", i) if c == NC - 1 else None)

        def to_edges(t, c):
            i = l * NT + t
            if c == 0:
                Q.wait(T, ("m8", i), ("st32", i), *([("q5", i - 1)] if i > NT else []))
            Q.op(T, lambda e: e.matmul(p_q[:, c * 48:(c + 1) * 48], ST16[:, c * P:(c + 1) * P], SM3,
                                       start=True, stop=True), ("sme", i) if c == NC - 1 else None)

        def exp(t):
            i = l * NT + t
            Q.wait(S, ("u5", i))
            Q.op(S, lambda e: e.activation(GB[t % NG][:, :, HALF:HALF + NH], U5[:, :, 0:NH], ACT.Exp), ("exp", i))

        def weigh(t, c0, c1):
            v = Thread(0.0, 0.15) if c0 else Thread(0.75, 1.0)
            i, s = l * NT + t, t % NG
            for c in range(c0, c1):
                j = i * NC + c
                row = GB[s][:, c, :]
                p = row[:, HALF:HALF + NH]
                both = row.rearrange("p (a o) -> p a o", a=2)[:, :, 0:HALF]
                if NH == 1:
                    fn = lambda e, both=both, p=p: e.tensor_scalar(both, both, p, None, ALU.mult)
                else:
                    def fn(e, both=both, p=p):
                        both = both.rearrange("p a (h o) -> p a h o", o=F)
                        weight = p.rearrange("p (a h) -> p a h", a=2).unsqueeze(3).broadcast_to([P, 2, NH // 2, F])
                        return e.tensor_tensor(both, both, weight, ALU.mult)
                v(fn, ("exp", i), key=("pgc", j), dep=False)
            return v

        def sums(t, c):
            i, s = l * NT + t, t % NG
            j = i * NC + c
            num = p_num[i % 2]
            if l == 0:
                sums_apart(t, c)
                return
            if c == 0:
                Q.wait(T, ("sel", i), ("y", i - 2))
            Q.wait(T, ("pgc", j))
            first, last = c == 0, c == NC - 1
            both = [(num[:, 0, 0:HALF + 8], GB[s][:, c, 0:HALF + 8]), (num[:, 1, 0:HALF], GB[s][:, c, HALF + 8:ROW])]
            for k, (to, rhs) in enumerate(both):
                Q.op(T, lambda e, to=to, rhs=rhs: e.matmul(to, SEL[i % 4][:, c * P:(c + 1) * P], rhs, start=first, stop=last),
                     ("used", i, c) if k == len(both) - 1 else None)
            if last:
                Q.marks["num", i] = Q.marks["used", i, c]

        def finish(t):
            v = Thread(0.22, 0.6 if l == 3 else 0.3) if l else Thread()
            i = l * NT + t
            num = p_num[i % 2][:, :, 0:HALF]
            x = X[:, t, :]
            two = lambda b: b.rearrange("p (a o) -> p a o", a=2)
            if l == 0:
                v(lambda e: e.scalar_tensor_tensor(Y, p_num[i % 2][:, 0, :], RDEG[:, t:t + 1], VT[t % 2], ALU.mult, ALU.add),
                  ("num", i), *done(("vin", t), t), key=("y", i))
                v(lambda e: e.scalar_tensor_tensor(x, Y, 0.0, x, ALU.max, ALU.add))
            else:
                v(lambda e: e.tensor_scalar(rden[:, 0:NH], p_num[i % 2][:, 0, HALF:HALF + NH], 1e-30, None, ALU.max), ("num", i),
                  *([("y", i - 1)] if i > NT else []))
                v(lambda e: e.reciprocal(rden[:, 0:NH], rden[:, 0:NH]), key=("rc", i))
                if l == 3:
                    out = VT[t % 2]
                    v(lambda e: e.scalar_tensor_tensor(two(out), num, rden[:, 0:1], two(x), ALU.mult, ALU.add),
                      *(done(("out", t - 2), t - 2) if t >= 2 else []), key=("y", i))
                    return [v]
                head, v = v, Thread(0.42, 1.0)
                if l == 2:
                    v(lambda e: e.scalar_tensor_tensor(x, Y, 0.0, x, ALU.max, ALU.add), ("y", i))
                    v(lambda e: e.scalar_tensor_tensor(x, Y2, -1.0, x, ALU.add, ALU.add), ("elu", i), key=("xd", i))
                else:
                    v(lambda e: e.tensor_tensor(x, x, Y, ALU.add), ("y", i), key=("xd", i))
            m = i + NT
            st = small[m % 2]
            v(lambda e: e.bn_stats(st[:, 0:6], x))
            v(lambda e: e.bn_aggr(st[:, 6:8], st[:, 0:6]))
            for k, fn in enumerate(rsqrt_steps(st[:, 8:9], st[:, 7:8], st[:, 13:14], st[:, 14:15], False)):
                v(fn, *([("h", m - 2)] if k == 1 else []))
            v(lambda e: e.scalar_tensor_tensor(st[:, 9:10], st[:, 6:7], -1.0, st[:, 8:9], ALU.mult, ALU.mult), key=("ln", m))
            return [head, v] if l else [v]

        def shares(t):
            i = l * NT + t
            Q.wait(S, ("rc", i), *([("xd", i - 1)] if i - 1 >= NT else []))
            for h in range(NH):
                a, b = divmod(h * F, HALF)
                Q.op(S, lambda e, h=h, a=a, b=b: e.activation(Y[:, h * F:(h + 1) * F], p_num[i % 2][:, a, b:b + F], ACT.Copy,
                                                              scale=rden[:, h:h + 1]), ("y", i) if h == NH - 1 else None)
            if l == 2:
                Q.wait(S, ("y", i))
                Q.op(S, lambda e: e.activation(Y2, Y, ACT.Relu, scale=-1.0), ("neg", i))
                Q.wait(S, ("neg", i))
                Q.op(S, lambda e: e.activation(Y2, Y2, ACT.Exp, scale=-1.0), ("elu", i))

        def finish_out(t):
            i = l * NT + t
            if l == 3:
                out = VT[t % 2]
                Q.wait(SP, ("y", i))
                pieces(SP, lambda a, b: dr["out"][t * P + a:t * P + b, :], lambda a, b: out[a:b, :], t, f"out{t % 2}", ("out", t))
                return
            m = i + NT
            node_h(t, m, small[m % 2][:, 8:9], small[m % 2][:, 9:10], ("ln", m))

        def products(t, k):
            n = rows(t)
            m = (l + 1) * NT + t
            w, ht = WL[l % 2], HT[m % 2]
            if k == 0:
                Q.wait(T, ("ht", m), ("w", l + 1, 0), ("w", l + 1, 1), ("we", l + 1), ("wo", m - 1))
            for a in range(2):
                Q.op(T, lambda e, a=a: e.matmul(p_wh[0:n, a, :], ht[:, k, 0:n], w[:, k, a, :], start=k == 0, stop=k == 3),
                     ("proj", m) if k == 3 and a == 1 else None)

        def products_out(t):
            n = rows(t)
            m = (l + 1) * NT + t
            buf = WO[t % 2]
            Q.wait(S, ("proj", m), "sm0")
            if t >= 2:
                Q.wait(S, *done(("tout", l + 1, t - 2), t - 2))
            else:
                Q.wait(S, *[k for u in (NT - 2, NT - 1) for k in done(("tout", l, u), u)])
            Q.op(S, lambda e: e.activation(buf.rearrange("p (a o) -> p a o", a=2)[0:n, :, :], p_wh[0:n, :, :], ACT.Copy), ("wo1", m))
            Q.op(S, lambda e: e.activation(SM[0:n, (l + 1) % 2, t, 0:8], p_wh[0:n, 1, HALF:HALF + 8], ACT.Copy), ("wo", m))
            Q.marks["sm", l + 1, t] = Q.marks["wo", m]
            Q.wait(SP, ("wo1", m))
            pieces(SP, lambda a, b: dr["T"][l + 1][t * P + a:t * P + b, :], lambda a, b: buf[a:b, 0:ROW], t, f"to{t % 2}", ("tout", l + 1, t))

        def load_v(t):
            if t >= 2:
                Q.wait(SP, ("y", t - 2))
            else:
                Q.wait(SP, "vpad", *[k for u in range(NT) for k in done(("vout", 0, u), u)])
            pieces(SP, lambda a, b: VT[t % 2][a:b, :], lambda a, b: dr["V"][t * P + a:t * P + b, :], t, f"v{t % 2}", ("vin", t))

        APART = (1,2,3,4)
        more = l < 3
        early = int(0 < l)
        la, lb, ls, le, lh, lp = (0, 1, 2, 3, 4, 5) if l else (0, 0, 0, 1, 2, 2)
        for t in range(NT):
            gather(t)
        sel(0)
        if l == 0:
            load_v(0)
            for c in APART[:2]:
                high(0, c)
        elif early:
            merged(Q, scores(0))
        for r in range(NT + lp + 1):
            on = lambda d: 0 <= r - d < NT
            att = lambda d: l > 0 and on(d)
            if on(ls):
                sums(r - ls, 0)
            if more and on(lh) and l == 0:
                node_tr(r - lh, (l + 1) * NT + r - lh)
            for c in range(1, NC):
                if c == 1:
                    for b in range(NC if att(lb) else 0):
                        to_edges(r - lb, b)
                    for b in range(NC if att(la) else 0):
                        ell(r - la, b)
                if on(ls):
                    sums(r - ls, c)
                if more and on(lp):
                    products(r - lp, c - 1)
                if c == 2 and more and on(lh) and l:
                    node_tr(r - lh, (l + 1) * NT + r - lh)
            merged(Q, *([low(r, APART[:2], 0.0, 0.02), low(r, APART[2:], 0.15, 0.8)] if l == 0 and on(0) else []),
                   *(finish(r - le) if on(le) else []), *([weigh(r - lb, 0, 3)] if att(lb) else []), *([weigh(r - ls, 3, NC)] if att(ls) else []),
                   *([highest(r - la)] if att(la) else []), *([scores(r + early)] if att(la - early) else []),
                   *([less_highest(r - lb)] if att(lb) else []))
            if more and on(lh) and l == 0:
                node_ht(r - lh, (l + 1) * NT + r - lh, True)
            if l in (1, 2) and on(le):
                shares(r - le)
            if att(la):
                st32(r - la)
            if att(lb):
                exp(r - lb)
            for c in APART[2:] if l == 0 and on(0) else ():
                high(r, c)
            if r + 1 < NT:
                sel(r + 1)
            if more and on(lh) and l:
                node_ht(r - lh, (l + 1) * NT + r - lh, True)
            for c in APART[:2] if l == 0 and r + 1 < NT else ():
                high(r + 1, c)
            if on(le):
                finish_out(r - le)
            if more and on(lp):
                products_out(r - lp)
            if l == 0 and r + 1 < NT:
                load_v(r + 1)

        if more:
            m = (l + 1) * NT + NT - 1
            v = Thread()
            v(lambda e: e.tensor_reduce(hsum, HS, AX.X, ALU.add), ("ht", m))
            v(lambda e: e.tensor_scalar(hsum, hsum, 1.0 / N, None, ALU.mult), key=("hsum", l))
            merged(Q, v)
            Q.wait(T, ("hsum", l))
            for a in range(2):
                for k in range(4):
                    Q.op(T, lambda e, a=a, k=k: e.matmul(p_t[0:1, a * HALF:(a + 1) * HALF], hsum[:, k:k + 1], WL[l % 2][:, k, a, 0:HALF],
                                                         start=k == 0, stop=k == 3), ("mean", l) if k == 3 and a else None)
            Q.wait(S, ("mean", l), *([("meanout", l)] if l else ["mrowz"]))
            for a in range(2):
                Q.op(S, lambda e, a=a: e.activation(mrow[0:1, a * (HALF + 8):a * (HALF + 8) + HALF], p_t[0:1, a * HALF:(a + 1) * HALF],
                                                    ACT.Copy), ("mrow", l) if a else None)
            Q.wait(T, ("mrow", l))
            Q.wait(SP, ("mrow", l))
            Q.dma(SP, lambda e: e.dma_start(dr["T"][l + 1][N:N + 1, :], mrow[0:1, :]), "meanout", ("meanout", l + 1))

    for l in range(4):
        layer(l)
    Q.wait(SP, *[k for t in (NT - 2, NT - 1) for k in done(("out", t), t)], *[("pwout", k) for k in range(5)], "pbout")


_W = {"W_self": "L0_gnn_W_self", "b_self": "L0_gnn_b_self", "W_nb": "L0_gnn_W_nb", "b_nb": "L0_gnn_b_nb",
      "W_comb": "L0_gnn_W_comb", "b_comb": "L0_gnn_b_comb", "W1": "L1_gnn_W", "a1": "L1_gnn_a",
      "W2": "L2_gnn_W", "a2": "L2_gnn_a", "W3": "L3_gnn_W", "a30": "L3_gnn_a1", "a31": "L3_gnn_a2"}


def program(nc, ins, out):
    dr = {k: ins[v] for k, v in _W.items()}
    dr.update(x=ins["x"], adj=ins["adj"], out=out)
    with ExitStack() as ctx:
        def scratch(name, shape):
            return nc.dram_tensor(name, shape, FP32, kind="Internal").ap()
        dr["PW"] = scratch("PW", [5, P, 4 * D])
        dr["PB"] = scratch("PB", [1, D])
        dr["XS"] = scratch("XS", [3, N, D])
        dr["Y"] = scratch("Y", [N, D])
        dr["V"] = scratch("V", [N, D])
        dr["WH"] = scratch("WH", [N, D])
        dr["HT"] = scratch("HT", [4, P, N])
        dr["S"] = scratch("S", [N, 8])
        dr["T"] = [scratch(f"T{l}", [N + 1, ROW if l else D]) for l in range(4)]
        words = 47500
        arena = ctx.enter_context(nc.sbuf_tensor("arena", [P, words], FP32))
        misc = ctx.enter_context(nc.sbuf_tensor("misc", [P, 1536], FP32))
        sel = ctx.enter_context(nc.sbuf_tensor("sel", [P, 3, 640], F32R))
        parts = ctx.enter_context(nc.sbuf_tensor("parts", [P, 2, 2, D], F32R))
        flag = ctx.enter_context(nc.sbuf_tensor("flag", [P, 1], I32))
        psum = ctx.enter_context(nc.psum_tensor("psum", [P, 8, D], FP32))

        def f(o, n):
            return arena[:, o:o + n]
        g = {"f": f, "arena_words": words, "ident": misc[:, 0:128], "ones": misc[:, 128:256],
             "WE": misc[:, 256:448].rearrange("p (l k h) -> p l k h", l=3, k=4),
             "bcol": misc[:, 448:452], "small": misc[:, 460:500],
             "brow": misc[:, 512:1536].rearrange("p (a n) -> p a n", a=2),
             "flag": flag[:, :], "psum": psum, "sel": sel, "parts": parts,
             "ps": psum[:, 0, :], "ps2": psum[:, 1, :], "ps3": psum[:, 2, :]}

        def run(name, emit):
            with nc.Block(name) as block:
                for engine, on in zip(ENGINES, (block.sync, block.tensor, block.vector, block.scalar, block.gpsimd)):
                    on(lambda e, engine=engine: emit(e, engine))

        Q = Queues(nc, ctx)
        sparse(Q, nc, g, dr)
        run("edges", Q.emit)
        Dn = Turns(nc, ctx, "dense")
        chain_dense(Dn, nc, g, dr)

        def fallback(e, name):
            full = e.value_load(g["flag"][0:1, 0:1], min_val=0, max_val=1)
            with e.If(full == 1):
                Dn.emit(e, name)
        run("dense", fallback)


_INS = ["x", "adj", *_W.values()]


def kernel(**inputs):
    import numpy as _np
    import concourse.bacc as _bacc
    from concourse import mybir as _mybir
    from concourse.bass_utils import run_bass_kernel_spmd as _run

    nc = _bacc.Bacc("TRN2", target_bir_lowering=False, num_devices=1)
    arrays, args = {}, {}
    for name in _INS:
        a = _np.ascontiguousarray(inputs[name])
        arrays[f"in_{name}"] = a
        args[name] = nc.dram_tensor(f"in_{name}", a.shape, _mybir.dt.from_np(a.dtype), kind="ExternalInput").ap()
    out = nc.dram_tensor("out_0", (N, D), _mybir.dt.float32, kind="ExternalOutput").ap()
    program(nc, args, out)
    r = _run(nc, [arrays], core_ids=[0])
    return r.results[0]["out_0"]
```
